# Optimizing a Trainium2 kernel written in Bass

```python
import numpy as np
import jax
import jax.numpy as jnp

def _softmax(x, axis=-1):
    return jax.nn.softmax(x, axis=axis)

def _gelu(x):
    return jax.nn.gelu(x, approximate=True)

def _silu(x):
    return jax.nn.silu(x)

def _sigmoid(x):
    return jax.nn.sigmoid(x)

def _layernorm(x, axis=-1, eps=1e-05):
    m = jnp.mean(x, axis=axis, keepdims=True)
    v = jnp.var(x, axis=axis, keepdims=True)
    return (x - m) / jnp.sqrt(v + eps)

def _scatter_add(tgt, idx, src, axis=0):
    return tgt.at[idx].add(src)

def _segment_sum(src, seg, n):
    return jax.ops.segment_sum(src, seg, n)
kernel_name = 'mk_macaron_d1_jaxref_r8_ac4024'

def setup_inputs(seed: int=0):
    np.random.seed(seed)
    _w = jnp.asarray

    def _L0_attn_setup():
        import jax, jax.numpy as jnp
        import numpy as np
        MIN_RAD, MAX_RAD, EPS = (0.9, 0.999, 1e-08)

        def block_diag_linear(x, w, b):
            h, bw, _ = w.shape
            xb = x.reshape(x.shape[0], x.shape[1], h, bw)
            y = jnp.einsum('bthi,hij->bthj', xb, w) + b
            return y.reshape(x.shape)
        key = jax.random.key(seed)
        kx, kw1, kw2, ka = jax.random.split(key, 4)
        B, T, width, num_heads = (8, 512, 128, 8)
        bw = width // num_heads
        std = np.sqrt(1.0 / bw)
        x = jax.random.normal(kx, (B, T, width), dtype=jnp.float32)
        ig_w = std * jax.random.normal(kw1, (num_heads, bw, bw), dtype=jnp.float32)
        ig_b = jnp.zeros((num_heads, bw), dtype=jnp.float32)
        ag_w = std * jax.random.normal(kw2, (num_heads, bw, bw), dtype=jnp.float32)
        ag_b = jnp.zeros((num_heads, bw), dtype=jnp.float32)
        u = jax.random.uniform(ka, (width,), dtype=jnp.float32, minval=MIN_RAD ** 2 + EPS, maxval=MAX_RAD ** 2 + EPS)
        a_param = jnp.log(jnp.exp(-0.5 * jnp.log(u)) - 1.0)
        return {'x': x, 'ig_w': ig_w, 'ig_b': ig_b, 'ag_w': ag_w, 'ag_b': ag_b, 'a_param': a_param}
    _L0_attn_in = _L0_attn_setup()

    def _L0_ffn_setup():
        import jax, jax.numpy as jnp
        import numpy as np
        DIM = 128
        DEPTH = 2
        HEADS = 8
        DIM_HEAD = 64
        WINDOW = 64
        INNER = HEADS * DIM_HEAD
        HID = int(DIM * 4 * 2 / 3)
        B, N = (2, 1024)
        QK_SCALE = 8.0

        def shift_token(t):
            t1, t2 = jnp.split(t, 2, axis=-1)
            t2 = jnp.pad(t2, ((0, 0), (1, 0), (0, 0)))[:, :-1]
            return jnp.concatenate([t1, t2], axis=-1)

        def l2norm(t):
            return t / jnp.clip(jnp.linalg.norm(t, axis=-1, keepdims=True), 1e-12)

        def rotate_half(x):
            x1, x2 = jnp.split(x, 2, axis=-1)
            return jnp.concatenate([-x2, x1], axis=-1)

        def rotary_xpos(q, k):
            n = q.shape[-2]
            half_idx = jnp.arange(0, DIM_HEAD, 2, dtype=jnp.float32)
            inv_freq = 1.0 / 10000.0 ** (half_idx / DIM_HEAD)
            t = jnp.arange(n, dtype=jnp.float32)
            freqs = t[:, None] * inv_freq[None, :]
            freqs = jnp.concatenate([freqs, freqs], axis=-1)
            base = (half_idx + 0.4 * DIM_HEAD) / (1.4 * DIM_HEAD)
            power = (t - n // 2) / float(WINDOW // 2)
            scale = base[None, :] ** power[:, None]
            scale = jnp.concatenate([scale, scale], axis=-1)
            cos, sin = (jnp.cos(freqs), jnp.sin(freqs))
            q = q * cos * scale + rotate_half(q) * sin * scale
            k = k * cos / scale + rotate_half(k) * sin / scale
            return (q, k)

        def local_attention(q, k, v):
            b, h, n, d = q.shape
            w = n // WINDOW
            bq = q.reshape(b, h, w, WINDOW, d) * QK_SCALE
            bk = k.reshape(b, h, w, WINDOW, d)
            bv = v.reshape(b, h, w, WINDOW, d)

            def look_around(t):
                p = jnp.pad(t, ((0, 0), (0, 0), (1, 0), (0, 0), (0, 0)))
                return jnp.concatenate([p[:, :, :w], p[:, :, 1:]], axis=3)
            bk, bv = (look_around(bk), look_around(bv))
            bt = jnp.arange(n).reshape(w, WINDOW)
            btp = jnp.pad(bt, ((1, 0), (0, 0)), constant_values=-1)
            btk = jnp.concatenate([btp[:w], btp[1:]], axis=1)
            sim = jnp.einsum('bhwid,bhwjd->bhwij', bq, bk)
            i = bt[:, :, None]
            j = btk[:, None, :]
            mask = (i < j) | (i > j + WINDOW) | (j == -1)
            sim = jnp.where(mask, -jnp.finfo(sim.dtype).max, sim)
            attn = jax.nn.softmax(sim, axis=-1)
            out = jnp.einsum('bhwij,bhwjd->bhwid', attn, bv)
            return out.reshape(b, h, n, d)

        def _layer(x, wqkv, qs, ksc, wo, lg, lb, w1, b1, w2, b2):
            b, n, _ = x.shape
            h = shift_token(x)
            qkv = h @ wqkv
            q, k, v = jnp.split(qkv, 3, axis=-1)
            to_heads = lambda t: t.reshape(b, n, HEADS, DIM_HEAD).transpose(0, 2, 1, 3)
            q, k, v = (to_heads(q), to_heads(k), to_heads(v))
            q = l2norm(q) * qs
            k = l2norm(k) * ksc
            q, k = rotary_xpos(q, k)
            o = local_attention(q, k, v)
            o = o.transpose(0, 2, 1, 3).reshape(b, n, INNER)
            x = x + o @ wo
            h = shift_token(x)
            mu = h.mean(-1, keepdims=True)
            var = h.var(-1, keepdims=True)
            h = (h - mu) / jnp.sqrt(var + 1e-05) * lg + lb
            h = h @ w1 + b1
            a, g = jnp.split(h, 2, axis=-1)
            h = a * jax.nn.gelu(g, approximate=False)
            x = x + h @ w2 + b2
            return x
        key = jax.random.key(seed)
        ks = jax.random.split(key, 6)
        return {'x': jax.random.normal(ks[0], (B, N, DIM), jnp.float32), 'wqkv': jax.random.normal(ks[1], (DEPTH, DIM, 3 * INNER), jnp.float32) * 0.02, 'q_scale': jnp.ones((DEPTH, DIM_HEAD), jnp.float32), 'k_scale': jnp.ones((DEPTH, DIM_HEAD), jnp.float32), 'wo': jax.random.normal(ks[2], (DEPTH, INNER, DIM), jnp.float32) * 0.02, 'ln_g': jnp.ones((DEPTH, DIM), jnp.float32), 'ln_b': jnp.zeros((DEPTH, DIM), jnp.float32), 'w1': jax.random.normal(ks[3], (DEPTH, DIM, 2 * HID), jnp.float32) * 0.02, 'b1': jnp.zeros((DEPTH, 2 * HID), jnp.float32), 'w2': jax.random.normal(ks[4], (DEPTH, HID, DIM), jnp.float32) * 0.02, 'b2': jnp.zeros((DEPTH, DIM), jnp.float32)}
    _L0_ffn_in = _L0_ffn_setup()
    _d = {'L0_attn_x': _L0_attn_in['x'], 'L0_attn_ig_w': _L0_attn_in['ig_w'], 'L0_attn_ig_b': _L0_attn_in['ig_b'], 'L0_attn_ag_w': _L0_attn_in['ag_w'], 'L0_attn_ag_b': _L0_attn_in['ag_b'], 'L0_attn_a_param': _L0_attn_in['a_param'], 'L0_ffn_wqkv': _L0_ffn_in['wqkv'], 'L0_ffn_q_scale': _L0_ffn_in['q_scale'], 'L0_ffn_k_scale': _L0_ffn_in['k_scale'], 'L0_ffn_wo': _L0_ffn_in['wo'], 'L0_ffn_ln_g': _L0_ffn_in['ln_g'], 'L0_ffn_ln_b': _L0_ffn_in['ln_b'], 'L0_ffn_w1': _L0_ffn_in['w1'], 'L0_ffn_b1': _L0_ffn_in['b1'], 'L0_ffn_w2': _L0_ffn_in['w2'], 'L0_ffn_b2': _L0_ffn_in['b2']}
    _x0 = _d['L0_attn_x']
    _d['L0_attn_x'] = jax.random.normal(jax.random.fold_in(jax.random.key(seed), 1), (16, 512, 128), dtype=_x0.dtype)
    del _x0
    return _d

def reference(L0_attn_x, L0_attn_ig_w, L0_attn_ig_b, L0_attn_ag_w, L0_attn_ag_b, L0_attn_a_param, L0_ffn_wqkv, L0_ffn_q_scale, L0_ffn_k_scale, L0_ffn_wo, L0_ffn_ln_g, L0_ffn_ln_b, L0_ffn_w1, L0_ffn_b1, L0_ffn_w2, L0_ffn_b2):

    def _L0_attn_ref(x, ig_w, ig_b, ag_w, ag_b, a_param):
        import jax, jax.numpy as jnp
        import numpy as np
        MIN_RAD, MAX_RAD, EPS = (0.9, 0.999, 1e-08)

        def block_diag_linear(x, w, b):
            h, bw, _ = w.shape
            xb = x.reshape(x.shape[0], x.shape[1], h, bw)
            y = jnp.einsum('bthi,hij->bthj', xb, w) + b
            return y.reshape(x.shape)
        gate_x = jax.nn.sigmoid(block_diag_linear(x, ig_w, ig_b))
        gate_a = jax.nn.sigmoid(block_diag_linear(x, ag_w, ag_b))
        log_a = -8.0 * gate_a * jax.nn.softplus(a_param)
        a = jnp.exp(log_a)
        a2 = jnp.exp(2.0 * log_a)
        gated_x = x * gate_x
        multiplier = jnp.sqrt(jnp.clip(1.0 - a2, 1e-07))
        normed_x = gated_x * multiplier
        B, T, D = x.shape
        p = jnp.cumprod(a, axis=1)
        p_prefix = jnp.concatenate([jnp.ones((B, 1, D), x.dtype), p[:, :-1]], axis=1)
        p_prefix = jnp.clip(p_prefix, 1e-07)
        w = normed_x / p_prefix
        S = jnp.cumsum(w, axis=1)
        h = p_prefix * S
        return h

    def _L0_ffn_ref(x, wqkv, q_scale, k_scale, wo, ln_g, ln_b, w1, b1, w2, b2):
        import jax, jax.numpy as jnp
        import numpy as np
        DIM = 128
        DEPTH = 2
        HEADS = 8
        DIM_HEAD = 64
        WINDOW = 64
        INNER = HEADS * DIM_HEAD
        HID = int(DIM * 4 * 2 / 3)
        B, N = (2, 1024)
        QK_SCALE = 8.0

        def shift_token(t):
            t1, t2 = jnp.split(t, 2, axis=-1)
            t2 = jnp.pad(t2, ((0, 0), (1, 0), (0, 0)))[:, :-1]
            return jnp.concatenate([t1, t2], axis=-1)

        def l2norm(t):
            return t / jnp.clip(jnp.linalg.norm(t, axis=-1, keepdims=True), 1e-12)

        def rotate_half(x):
            x1, x2 = jnp.split(x, 2, axis=-1)
            return jnp.concatenate([-x2, x1], axis=-1)

        def rotary_xpos(q, k):
            n = q.shape[-2]
            half_idx = jnp.arange(0, DIM_HEAD, 2, dtype=jnp.float32)
            inv_freq = 1.0 / 10000.0 ** (half_idx / DIM_HEAD)
            t = jnp.arange(n, dtype=jnp.float32)
            freqs = t[:, None] * inv_freq[None, :]
            freqs = jnp.concatenate([freqs, freqs], axis=-1)
            base = (half_idx + 0.4 * DIM_HEAD) / (1.4 * DIM_HEAD)
            power = (t - n // 2) / float(WINDOW // 2)
            scale = base[None, :] ** power[:, None]
            scale = jnp.concatenate([scale, scale], axis=-1)
            cos, sin = (jnp.cos(freqs), jnp.sin(freqs))
            q = q * cos * scale + rotate_half(q) * sin * scale
            k = k * cos / scale + rotate_half(k) * sin / scale
            return (q, k)

        def local_attention(q, k, v):
            b, h, n, d = q.shape
            w = n // WINDOW
            bq = q.reshape(b, h, w, WINDOW, d) * QK_SCALE
            bk = k.reshape(b, h, w, WINDOW, d)
            bv = v.reshape(b, h, w, WINDOW, d)

            def look_around(t):
                p = jnp.pad(t, ((0, 0), (0, 0), (1, 0), (0, 0), (0, 0)))
                return jnp.concatenate([p[:, :, :w], p[:, :, 1:]], axis=3)
            bk, bv = (look_around(bk), look_around(bv))
            bt = jnp.arange(n).reshape(w, WINDOW)
            btp = jnp.pad(bt, ((1, 0), (0, 0)), constant_values=-1)
            btk = jnp.concatenate([btp[:w], btp[1:]], axis=1)
            sim = jnp.einsum('bhwid,bhwjd->bhwij', bq, bk)
            i = bt[:, :, None]
            j = btk[:, None, :]
            mask = (i < j) | (i > j + WINDOW) | (j == -1)
            sim = jnp.where(mask, -jnp.finfo(sim.dtype).max, sim)
            attn = jax.nn.softmax(sim, axis=-1)
            out = jnp.einsum('bhwij,bhwjd->bhwid', attn, bv)
            return out.reshape(b, h, n, d)

        def _layer(x, wqkv, qs, ksc, wo, lg, lb, w1, b1, w2, b2):
            b, n, _ = x.shape
            h = shift_token(x)
            qkv = h @ wqkv
            q, k, v = jnp.split(qkv, 3, axis=-1)
            to_heads = lambda t: t.reshape(b, n, HEADS, DIM_HEAD).transpose(0, 2, 1, 3)
            q, k, v = (to_heads(q), to_heads(k), to_heads(v))
            q = l2norm(q) * qs
            k = l2norm(k) * ksc
            q, k = rotary_xpos(q, k)
            o = local_attention(q, k, v)
            o = o.transpose(0, 2, 1, 3).reshape(b, n, INNER)
            x = x + o @ wo
            h = shift_token(x)
            mu = h.mean(-1, keepdims=True)
            var = h.var(-1, keepdims=True)
            h = (h - mu) / jnp.sqrt(var + 1e-05) * lg + lb
            h = h @ w1 + b1
            a, g = jnp.split(h, 2, axis=-1)
            h = a * jax.nn.gelu(g, approximate=False)
            x = x + h @ w2 + b2
            return x
        for l in range(DEPTH):
            x = _layer(x, wqkv[l], q_scale[l], k_scale[l], wo[l], ln_g[l], ln_b[l], w1[l], b1[l], w2[l], b2[l])
        return x
    x = L0_attn_x
    x = x + 0.5 * _L0_ffn_ref(_layernorm(x, axis=-1), L0_ffn_wqkv, L0_ffn_q_scale, L0_ffn_k_scale, L0_ffn_wo, L0_ffn_ln_g, L0_ffn_ln_b, L0_ffn_w1, L0_ffn_b1, L0_ffn_w2, L0_ffn_b2)
    x = x + _L0_attn_ref(_layernorm(x, axis=-1), L0_attn_ig_w, L0_attn_ig_b, L0_attn_ag_w, L0_attn_ag_b, L0_attn_a_param)
    x = x + 0.5 * _L0_ffn_ref(_layernorm(x, axis=-1), L0_ffn_wqkv, L0_ffn_q_scale, L0_ffn_k_scale, L0_ffn_wo, L0_ffn_ln_g, L0_ffn_ln_b, L0_ffn_w1, L0_ffn_b1, L0_ffn_w2, L0_ffn_b2)
    return x

_drawn_inputs = setup_inputs


def setup_inputs(seed=0):
    import zlib

    import numpy as np

    out = dict(_drawn_inputs(seed))
    spreads = {'L0_attn_ig_b': (0.0, 0.326),
     'L0_attn_ag_b': (0.0, 0.324),
     'L0_ffn_q_scale': (1.0, 0.6),
     'L0_ffn_k_scale': (1.0, 0.6),
     'L0_ffn_ln_g': (1.0, 0.6),
     'L0_ffn_ln_b': (0.0, 0.8),
     'L0_ffn_b1': (0.0, 0.8),
     'L0_ffn_b2': (0.0, 0.378)}
    factors = {'L0_ffn_w1': 8.0, 'L0_ffn_w2': 5.888}
    for name, (base, spread) in spreads.items():
        noise = np.random.default_rng([zlib.crc32(name.encode()), seed]).standard_normal(out[name].shape)
        drawn = base * np.exp(spread * noise) if base else spread * noise
        out[name] = jnp.asarray(drawn.astype(out[name].dtype))
    for name, factor in factors.items():
        out[name] = (out[name] * factor).astype(out[name].dtype)
    return out
```

```python
from contextlib import ExitStack
from itertools import count

import numpy as np

import concourse.bass as bass
from concourse import mybir

F32 = mybir.dt.float32
BF16 = mybir.dt.bfloat16
ALU = mybir.AluOpType
ACT = mybir.ActivationFunctionType
AX = mybir.AxisListType

P = 128
SEQS, TOKENS, DIM = 16, 512, 128
TPS = TOKENS // P
HEADS, DH, WINDOW = 8, 64, 64
INNER = HEADS * DH
HID = int(DIM * 4 * 2 / 3)
HIDP = 3 * P
LAYERS = 2
TILES = LAYERS * SEQS * TPS
ITERS = LAYERS * SEQS
FILL = 4
DRAIN = 3
YCALL = 2 * SEQS * TPS + TILES
BLOCKS = 8
AHEAD = 4
QK_SCALE = 8.0
EPS = 1e-5
MASKED = -1e30
LOWEST = -3.0e38

C_IDENT, C_DOWN, C_FROM_PREV, C_UP, C_FROM_NEXT, C_MASK, C_FIRST, C_ROPE = (
    0, 128, 256, 384, 512, 640, 896, 1024)
C_ALL = C_ROPE + 2 * TPS * 2 * DH


def shape_constants():
    c = np.zeros((P, C_ALL), np.float32)
    i = np.arange(P)
    c[i, C_IDENT + i] = 1.0
    c[i[:-1], C_DOWN + i[1:]] = 1.0
    c[P - 1, C_FROM_PREV] = 1.0
    c[i[1:], C_UP + i[:-1]] = 1.0
    c[0, C_FROM_NEXT + P - 1] = 1.0
    c[0, C_FIRST:C_FIRST + P] = 1.0
    qi = np.arange(WINDOW)[:, None]
    kj = np.arange(WINDOW)[None, :]
    own, prev = np.where(kj <= qi, 0.0, MASKED), np.where(kj >= qi, 0.0, MASKED)
    odd_rows = np.concatenate([prev, own], axis=1)
    first = np.concatenate([np.concatenate([own, np.full_like(prev, MASKED)], 1), odd_rows], 0)
    other = np.concatenate([np.concatenate([own, prev], 1), odd_rows], 0)
    c[:, C_MASK:C_MASK + P], c[:, C_MASK + P:C_MASK + 2 * P] = first, other
    half = np.arange(0, DH, 2, dtype=np.float32)
    inv = (np.float32(1.0) / np.float32(10000.0) ** (half / np.float32(DH))).astype(np.float32)
    pos = np.arange(TOKENS, dtype=np.float32)
    ang = (pos[:, None] * inv[None, :]).astype(np.float32).astype(np.float64)
    base = ((half + np.float32(0.4 * DH)) / np.float32(1.4 * DH)).astype(np.float64)
    scale = base[None, :] ** ((pos - TOKENS // 2) / float(WINDOW // 2))[:, None]
    cos, sin = np.cos(ang), np.sin(ang)
    rope = np.zeros((TOKENS, 2, 2, DH))
    for n, s in enumerate((scale * QK_SCALE, 1.0 / scale)):
        rope[:, 0, n] = np.concatenate([cos * s, cos * s], -1)
        rope[:, 1, n] = np.concatenate([sin * s, -sin * s], -1)
    rope = rope.reshape(TPS, P, 2, 2, DH).transpose(1, 2, 0, 3, 4)
    c[:, C_ROPE:] = rope.reshape(P, -1)
    return c


class Stage:

    def __init__(self, it, t, lag, regs):
        d = t - lag
        self.r, self.back = d % TPS, d // TPS
        self.k = TPS * (it + self.back) + self.r
        self.live = not isinstance(self.k, int) or 0 <= self.k < TILES
        if self.live:
            self.seq, self.layer = regs(self.back)
        self.par = self.r % 2


def due(value):
    return max(value, 0) if isinstance(value, int) else value


def build(nc, x_in, ig_w, ig_b, ag_w, ag_b, a_param, wqkv_in, q_scale, k_scale, wo_in, ln_g, ln_b, w1_in, b1_in,
          w2_in, b2_in, consts, out):
    with ExitStack() as ctx:
        def sb(name, shape, dt=F32):
            return ctx.enter_context(nc.sbuf_tensor(name, shape, dt))

        def ps(name, cols):
            return ctx.enter_context(nc.psum_tensor(name, [P, cols], F32))

        def sem(name):
            return ctx.enter_context(nc.semaphore(name))

        xs = sb("xs", [P, SEQS, TPS, DIM])
        ys = sb("ys", [P, SEQS, TPS, DIM])
        wqkv = sb("wqkv", [P, LAYERS, 3 * INNER])
        wo = sb("wo", [P, LAYERS, INNER // P, DIM])
        w1 = sb("w1", [P, LAYERS, 2 * HID])
        w2 = sb("w2", [P, LAYERS, 3, DIM])
        b1s = sb("b1s", [P, LAYERS, 2 * HID], BF16)
        b2s = sb("b2s", [P, LAYERS, DIM], BF16)
        ones_bf = sb("ones_bf", [P, P], BF16)
        cst = sb("cst", [P, C_ROPE])
        rope = sb("rope", [P, LAYERS, 2, TPS, 2, DH])
        gate_w = sb("gate_w", [P, 2, DIM])
        gate_b = sb("gate_b", [P, 2])
        decay = sb("decay", [P, 8])
        lnp_w = sb("lnp_w", [P, LAYERS, 2])
        qk_scale = sb("qk_scale", [P, LAYERS, 2, DH])
        scratch = sb("scratch", [P, 8])
        table_scratch = sb("table_scratch", [P, 8])
        zero_col = sb("zero_col", [P, 1])
        half_neg = sb("half_neg", [P, 16])
        yst = sb("yst", [P, 2, DIM])
        hT = sb("hT", [P, TOKENS + 1])
        mT = sb("mT", [P, TOKENS + 1])
        sq = sb("sq", [P, 2 * INNER])
        rot = sb("rot", [P, 2, 2 * INNER])
        rsin = sb("rsin", [P, 2, 2 * INNER])
        ss = sb("ss", [P, 2, 2 * HEADS])
        rn = sb("rn", [P, 2, 2 * HEADS])
        QT = sb("QT", [P, 4, TPS, P])
        KT = sb("KT", [P, 4, TPS, P])
        Vb = sb("Vb", [P, TPS, HEADS, DH + 1])
        Va = sb("Va", [P, TPS, HEADS, DH + 1])
        S = sb("S", [P, 2, 2, 4, P])
        mx = sb("mx", [P, 2, 8])
        nmx = sb("nmx", [P, 2, 8])
        PT = sb("PT", [P, 2, 4, P])
        rc = sb("rc", [P, 4])
        O = sb("O", [P, 2, INNER])
        OT = sb("OT", [P, 4, P])
        tup = sb("tup", [P, TPS, 12])
        tupB = sb("tupB", [P, TPS + 1, 6])
        mv = sb("mv", [P, TPS, 2])
        mr = sb("mr", [P, TPS + 1, 2])
        lnp = sb("lnp", [P, TPS, 2, 2])
        before = sb("before", [P, 2])
        nb = sb("nb", [P, TPS, DIM])
        gl = sb("gl", [P, HID])
        gg = sb("gg", [P, 2, HIDP])
        gT = sb("gT", [P, 3, P])
        pst = sb("pst", [P, 2, TPS, 6])
        pmv = sb("pmv", [P, 2, TPS, 2])
        prs = sb("prs", [P, 2, TPS])

        ident = cst[:, C_IDENT:C_IDENT + P]
        down, from_prev = cst[:, C_DOWN:C_DOWN + P], cst[:, C_FROM_PREV:C_FROM_PREV + P]
        first_row = cst[:, C_FIRST:C_FIRST + P]
        up, from_next = cst[:, C_UP:C_UP + P], cst[:, C_FROM_NEXT:C_FROM_NEXT + P]

        B01, B2, B3 = ps("B01", 1024), ps("B2", 512), ps("B3", 512)
        B45, B6, B7 = ps("B45", 1024), ps("B6", 512), ps("B7", 512)

        turns = range(2)
        R_in = [sq[:, 512 * u:512 * (u + 1)] for u in turns]
        R_nT, R_gx = [rot[:, u, 0:512] for u in turns], [rot[:, u, 512:1024] for u in turns]
        R_ga, R_a = [rsin[:, u, 0:512] for u in turns], [rsin[:, u, 512:1024] for u in turns]
        R_a2, R_mult = ([S[:, u, e].rearrange("p j n -> p (j n)") for u in turns] for e in range(2))
        QTf, KTf = QT[:].rearrange("p c t n -> p (c t n)"), KT[:].rearrange("p c t n -> p (c t n)")
        R_p = [QTf[:, 1024 * u:1024 * u + TOKENS + 1] for u in turns]
        R_pc = [KTf[:, 1024 * u:1024 * u + 512] for u in turns]
        R_rec = [KTf[:, 1024 * u + 512:1024 * u + 1024] for u in turns]
        R_w, R_S = [PT[:, u].rearrange("p j n -> p (j n)") for u in turns], [O[:, u] for u in turns]

        load_w, load_x, stored = sem("load_w"), sem("load_x"), sem("stored")
        set_v, set_p, set_e, set_d, phase = sem("set_v"), sem("set_p"), sem("set_e"), sem("set_d"), sem("phase")
        pe_qk, pe_v, pe_qT, pe_kT = sem("pe_qk"), sem("pe_v"), sem("pe_qT"), sem("pe_kT")
        pe_S, pe_PT, pe_O, pe_OT = sem("pe_S"), sem("pe_PT"), sem("pe_O"), sem("pe_OT")
        pe_wo, pe_yT, pe_nT, pe_h = sem("pe_wo"), sem("pe_yT"), sem("pe_nT"), sem("pe_h")
        pe_gT, pe_w2, pe_st1, pe_st2 = sem("pe_gT"), sem("pe_w2"), sem("pe_st1"), sem("pe_st2")
        pe_lr_nT, pe_lr_g, pe_lr_h = sem("pe_lr_nT"), sem("pe_lr_g"), sem("pe_lr_h")
        dv_y, dv_rope, dv_ss, dv_vc = sem("dv_y"), sem("dv_rope"), sem("dv_ss"), sem("dv_vc")
        dv_mx, dv_sm, dv_rc, dv_O = sem("dv_mx"), sem("dv_sm"), sem("dv_rc"), sem("dv_O")
        dv_hT, dv_mT, dv_gg, dv_r1 = sem("dv_hT"), sem("dv_mT"), sem("dv_gg"), sem("dv_r1")
        dv_bn, dv_ln, dv_tc, dv_ag = sem("dv_bn"), sem("dv_ln"), sem("dv_tc"), sem("dv_ag")
        dv_lp, dv_agg, dv_pag, dv_sum = sem("dv_lp"), sem("dv_agg"), sem("dv_pag"), sem("dv_sum")
        dv_pa, dv_pst, dv_x, dv_z = sem("dv_pa"), sem("dv_pst"), sem("dv_x"), sem("dv_z")
        dv_lr_m, dv_lr_p, dv_lr_pc, dv_lr_rec = sem("dv_lr_m"), sem("dv_lr_p"), sem("dv_lr_pc"), sem("dv_lr_rec")
        dv_lr_w, dv_lr_S, dv_lr_h, dv_lr_x = sem("dv_lr_w"), sem("dv_lr_S"), sem("dv_lr_h"), sem("dv_lr_x")
        ac_sq, ac_v, ac_qT, ac_kT = sem("ac_sq"), sem("ac_v"), sem("ac_qT"), sem("ac_kT")
        ac_P, ac_PT, ac_gl, ac_OT = sem("ac_P"), sem("ac_PT"), sem("ac_gl"), sem("ac_OT")
        ac_gT, ac_lr_in, ac_lr_nT, ac_lr_g = sem("ac_gT"), sem("ac_lr_in"), sem("ac_lr_nT"), sem("ac_lr_g")
        ac_lr_a, ac_lr_m = sem("ac_lr_a"), sem("ac_lr_m")
        po_rn, po_add, po_q, po_rs = sem("po_rn"), sem("po_add"), sem("po_q"), sem("po_rs")
        po_prs, po_y, po_lr_nx, po_lr_nm = sem("po_prs"), sem("po_y"), sem("po_lr_nx"), sem("po_lr_nm")

        def N(call, k, per=1, j=1):
            if isinstance(k, int):
                k = min(k, TILES - 1)
            return due(per * (TILES * call + k) + j)

        def Y(call, k):
            if isinstance(k, int):
                k = min(k, TILES - 1)
            return due(YCALL * call + SEQS * TPS + k + 1)

        def seq_live(it):
            return not isinstance(it, int) or 0 <= it - 2 < ITERS

        def J(call, j):
            return due(ITERS * call + j + 1)

        def barrier(eng, n):
            eng.drain().then_inc(phase, 1)
            eng.wait_ge(phase, 4 * n)

        scratch_turn = count()

        def settle(eng):
            if eng is nc.tensor:
                eng.matmul(B45[:, 0:64], ones_bf[:], ones_bf[:, 0:64], start=True, stop=True)
            else:
                n = next(scratch_turn) % 8
                eng.memset(scratch[:, n:n + 1], 0.0)

        def tile_of(buf, st):
            if isinstance(st.seq, int):
                return buf[:, st.seq, st.r, :]
            return buf[:, bass.ds(st.seq, 1), st.r, :].rearrange("p a d -> p (a d)")

        def seq_tile(buf, q, t):
            if isinstance(q, int):
                return buf[:, q, t, :]
            return buf[:, bass.ds(q, 1), t, :].rearrange("p a d -> p (a d)")

        def of_layer(buf, st, a, b):
            n = len(buf.shape)
            flat = buf[:] if n == 3 else buf[:].rearrange("p l c d -> p l (c d)")
            if isinstance(st.layer, int):
                return flat[:, st.layer, a:b]
            return flat[:, bass.ds(st.layer, 1), a:b].rearrange("p a d -> p (a d)")

        def rope_of(st, cs, n):
            if isinstance(st.layer, int):
                v = rope[:, st.layer, cs, st.r, n, :].unsqueeze(1)
            else:
                v = rope[:, bass.ds(st.layer, 1), cs, st.r, n, :]
            return v.broadcast_to([P, HEADS, DH])

        def pipeline(eng, slot, call):
            def regs_at(it):
                kept = {}

                def regs(back):
                    if isinstance(it, int):
                        return (it + back) % SEQS, (it + back) // SEQS
                    if back not in kept:
                        kept[back] = (eng.snap((it + back) % SEQS), eng.snap((it + back) // SEQS))
                    return kept[back]
                return regs

            def iteration(it, steady):
                regs = regs_at(it)
                for t in range(TPS):
                    slot(call, it, t, steady, lambda lag: Stage(it, t, lag, regs))

            slot(call, -1, TPS - 1, False, lambda lag: Stage(-1, TPS - 1, lag, regs_at(-1)))
            for it in range(FILL):
                iteration(it, False)
            with eng.Fori(FILL, ITERS - 1) as it:
                iteration(it, True)
            for it in range(ITERS - 1, ITERS + DRAIN):
                iteration(it, False)

        def recurrence(eng, step):
            for q in range(3):
                step(q, q % 2)
            with eng.Fori(0, 4) as i:
                step(2 * i + 3, 1)
                step(2 * i + 4, 0)
            for q in range(11, SEQS):
                step(q, q % 2)

        def within(q, first, last):
            return not isinstance(q, int) or first <= q <= last

        block = ctx.enter_context(nc.Block())
        x_t = x_in.rearrange("s (t p) d -> p s t d", p=P)
        o_t = out.rearrange("s (t p) d -> p s t d", p=P)
        n_weights = []

        @block.sync
        def _(sp):
            def load(dst, src):
                sp.dma_start(dst, src).then_inc(load_w, 16)
                n_weights.append(1)
            for q in range(4):
                sp.dma_start(xs[:, 4 * q:4 * q + 4].rearrange("p s t d -> p (s t) d"),
                             x_t[:, 4 * q:4 * q + 4].rearrange("p s t d -> p (s t) d")).then_inc(load_x, 16)
            load(cst[:], consts[:, 0:C_ROPE])
            for l in range(LAYERS):
                load(rope[:, l].rearrange("p a t n d -> p (a t n d)"), consts[:, C_ROPE:C_ALL])
                load(wqkv[:, l], wqkv_in[l])
                load(wo[:, l], wo_in[l].rearrange("(c p) d -> p c d", p=P))
                load(w1[:, l], w1_in[l])
                load(w2[:, l, 0:2], w2_in[l, 0:2 * P].rearrange("(c p) d -> p c d", p=P))
                load(lnp_w[:, l, 0:1], ln_g[l:l + 1].rearrange("a d -> d a"))
                load(lnp_w[:, l, 1:2], ln_b[l:l + 1].rearrange("a d -> d a"))
                load(qk_scale[:, l, 0], q_scale[l:l + 1].broadcast_to([P, DH]))
                load(qk_scale[:, l, 1], k_scale[l:l + 1].broadcast_to([P, DH]))
                load(sq[0:3, 0:2 * HID] if l == 0 else rot[0:3, 0, 0:2 * HID],
                     b1_in[l:l + 1].broadcast_to([3, 2 * HID]))
                load(rsin[0:3, 0, l * DIM:(l + 1) * DIM], b2_in[l:l + 1].broadcast_to([3, DIM]))
            sp.wait_ge(set_v, 1)
            for l in range(LAYERS):
                load(w2[0:HID - 2 * P, l, 2], w2_in[l, 2 * P:HID])
            bw = DIM // BLOCKS
            for n, (w, b) in enumerate(((ig_w, ig_b), (ag_w, ag_b))):
                for i in range(BLOCKS):
                    load(gate_w[i * bw:(i + 1) * bw, n, i * bw:(i + 1) * bw], w[i])
                load(gate_b[:, n:n + 1], b.rearrange("h (i a) -> (h i) a", a=1))
            load(decay[:, 0:1], a_param.rearrange("(d a) -> d a", a=1))
            for q in range(4):
                sp.wait_ge(dv_x, 4 + q + 1)
                sp.dma_start(o_t[:, 4 * q:4 * q + 4].rearrange("p s t d -> p (s t) d"),
                             xs[:, 4 * q:4 * q + 4].rearrange("p s t d -> p (s t) d")).then_inc(stored, 16)
            sp.wait_ge(stored, 64)

        W_ALL = 16 * len(n_weights)

        @block.tensor
        def _(pe):
            pe.wait_ge(load_w, W_ALL)
            pe.wait_ge(set_v, 2)
            for l in range(LAYERS):
                for n in range(2):
                    m = pe.matmul(B01[0:3, 512 * n:512 * n + HID] if l == 0 else B45[0:3, 512 * n:512 * n + HID],
                                  QT[:, 0, l, 0:3], w1[:, l, n * HID:(n + 1) * HID], start=True, stop=True)
            m.then_inc(set_e, 1)
            pe.wait_ge(set_v, 3)

            def slot(call, it, t, steady, at):
                g, a1, a2, a3, a4 = at(0), at(1), at(2), at(3), at(4)
                nxt, c10, c11, c12 = at(-1), at(10), at(11), at(12)
                k = g.k
                if g.live:
                    pe.wait_ge(dv_gg, N(call, k - 12))
                    if not steady:
                        pe.wait_ge(dv_rope, N(call, k - 1))
                        pe.wait_ge(ac_sq, N(call, k - 1, 2, 2))
                    pe.wait_ge(dv_hT, N(call, k))
                    h = hT[:, P * g.r:P * (g.r + 1)]
                    for n in range(2):
                        m = pe.matmul(B01[:, 512 * n:512 * (n + 1)], h, of_layer(wqkv, g, INNER * n, INNER * (n + 1)),
                                      start=True, stop=True)
                    m.then_inc(pe_qk, 1)
                    pe.wait_ge(dv_y, Y(call, k - 13))
                    if not steady:
                        pe.wait_ge(dv_mT, N(call, k - 11))
                    pe.matmul(B2[:, :], h, of_layer(wqkv, g, 2 * INNER, 3 * INNER), start=True, stop=True)\
                        .then_inc(pe_v, 1)
                if a1.live:
                    pe.wait_ge(po_q, N(call, a1.k))
                    pe.wait_ge(ac_gT, N(call, k - 13))
                    if not steady:
                        pe.wait_ge(ac_OT, N(call, k - 5))
                        pe.wait_ge(ac_kT, N(call, k - 2))
                    for c in range(4):
                        m = pe.transpose(B3[:, P * c:P * (c + 1)], rot[:, a1.par, P * c:P * (c + 1)], ident)
                    m.then_inc(pe_qT, 1)
                if a2.live:
                    pe.wait_ge(ac_qT, N(call, a2.k))
                    pe.wait_ge(ac_kT, N(call, a2.k))
                    pe.wait_ge(dv_sm, N(call, a2.k - 1))
                    if t == 1 and seq_live(it):
                        pe.wait_ge(dv_tc, J(call, it - 2))
                    if t == 2 and seq_live(it):
                        pe.wait_ge(dv_lp, J(call, it - 2))
                    settle(pe)
                    r = a2.r
                    for j in range(4):
                        for e in range(2):
                            rows = slice(64 * e, 64 * e + 64)
                            kh = KT[rows, j].rearrange("p t (w n) -> p (t w) n", n=WINDOW)
                            ka = kh[:, 0:8:7, :] if r == 0 else kh[:, 2 * r:(2 * r - 2 if r > 1 else 0):-1, :]
                            pe.matmul(B45[0:64, 512 * e + P * j:512 * e + P * (j + 1)], QT[rows, j, r, 0:64],
                                      ka, start=True, stop=True)
                            m = pe.matmul(B45[64:128, 512 * e + P * j:512 * e + P * (j + 1)], QT[rows, j, r, 64:128],
                                          KT[rows, j, r, :], start=True, stop=True)
                    m.then_inc(pe_S, 1)
                if a1.live:
                    pe.wait_ge(ac_qT, N(call, a1.k))
                    for c in range(4):
                        m = pe.transpose(B3[:, P * c:P * (c + 1)], rot[:, a1.par, INNER + P * c:INNER + P * (c + 1)],
                                         ident)
                    m.then_inc(pe_kT, 1)

                def probs_T(e):
                    pe.wait_ge(ac_P, N(call, a3.k, 2, 1 + e))
                    if e == 0:
                        pe.wait_ge(dv_r1, N(call, k - 5))
                    if e == 1 or not steady:
                        pe.wait_ge(ac_PT, N(call, a3.k, 2, e))
                    for j in range(4):
                        m = pe.transpose(B6[:, P * j:P * (j + 1)], S[:, a3.par, e, j, :], ident)
                    m.then_inc(pe_PT, 1)

                def times_v(e):
                    pe.wait_ge(ac_PT, N(call, a3.k, 2, 1 + e))
                    pe.wait_ge(dv_O, N(call, a3.k, 2, e))
                    pe.wait_ge(dv_vc, N(call, a3.k))
                    for j in range(4):
                        cols = slice((DH + 1) * j, (DH + 1) * (j + 1))
                        pe.matmul(B7[0:64, cols], PT[:, e, j, 0:64], Va[:, a3.r, 2 * j + e, :], start=True, stop=True)
                        m = pe.matmul(B7[64:128, cols], PT[:, e, j, 64:128], Vb[:, a3.r, 2 * j + e, :],
                                      start=True, stop=True)
                    m.then_inc(pe_O, 1)

                if a3.live:
                    probs_T(0)
                if c11.live:
                    pe.wait_ge(dv_mT, N(call, c11.k))
                    pe.wait_ge(dv_rope, N(call, k))
                    pe.wait_ge(ac_sq, N(call, k, 2, 2))
                    if not steady:
                        pe.wait_ge(dv_gg, N(call, c11.k - 1))
                    for n in range(2):
                        o = B01[:, 512 * n:512 * n + HID]
                        pe.matmul(o, ones_bf[:], of_layer(b1s, c11, HID * n, HID * (n + 1)), start=True, stop=False)
                        m = pe.matmul(o, mT[:, P * c11.r:P * (c11.r + 1)], of_layer(w1, c11, HID * n, HID * (n + 1)),
                                      start=False, stop=True)
                    m.then_inc(pe_h, 1)
                if a3.live:
                    times_v(0)
                    probs_T(1)
                if a4.live:
                    pe.wait_ge(dv_O, N(call, a4.k, 2, 2))
                    pe.wait_ge(ac_kT, N(call, k - 1))
                    if not steady:
                        pe.wait_ge(ac_gT, N(call, k - 13))
                    for c in range(4):
                        m = pe.transpose(B3[:, P * c:P * (c + 1)], O[:, a4.par, P * c:P * (c + 1)], ident)
                    m.then_inc(pe_OT, 1)
                if nxt.live or c10.live:
                    pe.wait_ge(ac_v, N(call, k))
                    if not steady:
                        pe.wait_ge(dv_y, Y(call, k - 13))
                        pe.wait_ge(dv_mT, N(call, k - 11))
                if nxt.live:
                    pe.wait_ge(po_y, N(call, nxt.k))
                    pe.transpose(B2[:, 0:P], yst[:, nxt.par, :], ident).then_inc(pe_yT, 1)
                if c10.live:
                    pe.wait_ge(dv_ln, N(call, c10.k))
                    if c10.r == 0:
                        pe.matmul(B2[:, 2 * P:2 * P + 2], first_row, before[:], start=True, stop=True)
                    pe.transpose(B2[:, P:2 * P], nb[:, c10.r, :], ident).then_inc(pe_nT, 1)
                if a3.live:
                    times_v(1)
                if t == 0 and seq_live(it):
                    j = it - 2
                    pe.wait_ge(dv_bn, N(call, TPS * j + TPS - 1))
                    pe.wait_ge(dv_sm, N(call, a2.k))
                    o = B45[:, 0:TPS * 6]
                    pe.matmul(o, down, tupB[:, 1:TPS + 1, :].rearrange("p t n -> p (t n)"), start=True, stop=False)
                    pe.matmul(o, from_prev, tupB[:, 0:TPS, :].rearrange("p t n -> p (t n)"), start=False, stop=True)\
                        .then_inc(pe_st1, 1)
                if t == 1 and seq_live(it):
                    j = it - 2
                    pe.wait_ge(po_rs, J(call, j))
                    pe.wait_ge(dv_sm, N(call, a2.k))
                    o = B45[:, 512:512 + TPS * 2]
                    pe.matmul(o, up, mr[:, 0:TPS, :].rearrange("p t n -> p (t n)"), start=True, stop=False)
                    pe.matmul(o, from_next, mr[:, 1:TPS + 1, :].rearrange("p t n -> p (t n)"), start=False, stop=True)\
                        .then_inc(pe_st2, 1)
                if c12.live:
                    pe.wait_ge(dv_gg, N(call, c12.k))
                    pe.wait_ge(ac_OT, N(call, k - 4))
                    if not steady:
                        pe.wait_ge(ac_kT, N(call, k - 1))
                        pe.wait_ge(ac_gT, N(call, k - 13))
                    for c in range(3):
                        m = pe.transpose(B3[:, P * c:P * (c + 1)], gg[:, c12.par, P * c:P * (c + 1)], ident)
                    m.then_inc(pe_gT, 1)
                if a4.live:
                    pe.wait_ge(ac_OT, N(call, a4.k))
                    pe.wait_ge(ac_PT, N(call, k - 3, 2, 2))
                    if not steady:
                        pe.wait_ge(dv_r1, N(call, k - 5))
                    for c in range(4):
                        m = pe.matmul(B6[:, 0:DIM], OT[:, c, :], of_layer(wo, a4, DIM * c, DIM * (c + 1)),
                                      start=(c == 0), stop=(c == 3))
                    m.then_inc(pe_wo, 1)
                if c12.live:
                    pe.wait_ge(ac_gT, N(call, c12.k))
                    pe.wait_ge(dv_mT, N(call, k - 10))
                    pe.wait_ge(dv_hT, N(call, k + 1))
                    if not steady:
                        pe.wait_ge(ac_v, N(call, k))
                        pe.wait_ge(dv_y, Y(call, k - 13))
                    o = B2[:, 0:DIM]
                    pe.matmul(o, ones_bf[:], of_layer(b2s, c12, 0, DIM), start=True, stop=False)
                    for c in range(3):
                        m = pe.matmul(o, gT[:, c, :], of_layer(w2, c12, DIM * c, DIM * (c + 1)),
                                      start=False, stop=(c == 2))
                    m.then_inc(pe_w2, 1)

            def rec_gates(q, u):
                bank, gbank = (B2, B3)[u], (B01, B45)[u]
                pe.wait_ge(ac_lr_in, q + 1)
                pe.wait_ge(ac_lr_nT, due(q - 1))
                for t in range(TPS):
                    m = pe.transpose(bank[:, P * t:P * (t + 1)], R_in[u][:, P * t:P * (t + 1)], ident)
                m.then_inc(pe_lr_nT, 1)
                pe.wait_ge(ac_lr_nT, q + 1)
                pe.wait_ge(ac_lr_g, due(q - 1))
                for n in range(2):
                    m = pe.matmul(gbank[:, TOKENS * n:TOKENS * (n + 1)], gate_w[:, n, :], R_nT[u], start=True, stop=True)
                m.then_inc(pe_lr_g, 1)

            def rec_back(q, u):
                pe.wait_ge(dv_lr_h, q + 1)
                pe.wait_ge(dv_lr_x, due(q - 1))
                for t in range(TPS):
                    m = pe.transpose((B6, B7)[u][:, P * t:P * (t + 1)], R_w[u][:, P * t:P * (t + 1)], ident)
                m.then_inc(pe_lr_h, 1)

            barrier(pe, 1)
            pipeline(pe, slot, 0)
            barrier(pe, 2)
            rec_gates(0, 0)

            def step(q, u):
                if within(q, 0, SEQS - 2):
                    rec_gates(q + 1, 1 - u)
                if within(q, 1, SEQS - 1):
                    rec_back(q - 1, 1 - u)

            recurrence(pe, step)
            rec_back(SEQS - 1, 1)
            barrier(pe, 3)
            pipeline(pe, slot, 1)

        @block.scalar
        def _(act):
            def copy(out_, in_):
                return act.activation(out_, in_, ACT.Copy)

            table_turn = count()

            def fetch_table(function):
                n = next(table_turn) % 8
                act.activation(table_scratch[:, n:n + 1], half_neg[:, 0:1], function)

            def slot(call, it, t, steady, at):
                g, a1, a2, a3, a4, c11, c12 = (at(n) for n in (0, 1, 2, 3, 4, 11, 12))
                k = g.k
                if g.live:
                    act.wait_ge(pe_qk, N(call, k))
                    act.wait_ge(dv_ss, N(call, k - 1))
                    for n in range(2):
                        act.activation(sq[:, 512 * n:512 * (n + 1)], B01[:, 512 * n:512 * (n + 1)], ACT.Square)\
                            .then_inc(ac_sq, 1)
                    act.wait_ge(pe_v, N(call, k))
                    act.wait_ge(pe_O, N(call, k - 4, 2, 2))
                    copy(Vb[:, g.r, :, 0:DH], B2[:].rearrange("p (h d) -> p h d", h=HEADS)).then_inc(ac_v, 1)
                if a1.live:
                    act.wait_ge(pe_qT, N(call, a1.k))
                    act.wait_ge(pe_S, N(call, a1.k - 4))
                    copy(QT[:, :, a1.r, :], B3[:].rearrange("p (c n) -> p c n", c=4)).then_inc(ac_qT, 1)
                    act.wait_ge(pe_kT, N(call, a1.k))
                    act.wait_ge(pe_S, N(call, a1.k - 3))
                    copy(KT[:, :, a1.r, :], B3[:].rearrange("p (c n) -> p c n", c=4)).then_inc(ac_kT, 1)

                def probs_T(e):
                    act.wait_ge(pe_PT, N(call, a3.k, 2, 1 + e))
                    act.wait_ge(pe_O, N(call, a3.k - 1, 2, 1 + e))
                    copy(PT[:, e].rearrange("p j n -> p (j n)"), B6[:]).then_inc(ac_PT, 1)

                if a3.live:
                    probs_T(0)
                if c11.live:
                    fetch_table(ACT.Gelu)
                    act.wait_ge(pe_h, N(call, c11.k))
                    act.wait_ge(dv_gg, N(call, c11.k - 1))
                    act.activation(gl[:], B01[:, 512:512 + HID], ACT.Gelu).then_inc(ac_gl, 1)
                if a3.live:
                    probs_T(1)
                if a4.live:
                    act.wait_ge(pe_OT, N(call, a4.k))
                    act.wait_ge(pe_wo, N(call, a4.k - 1))
                    copy(OT[:].rearrange("p c n -> p (c n)"), B3[:]).then_inc(ac_OT, 1)
                if a2.live:
                    fetch_table(ACT.Exp)
                if c12.live:
                    act.wait_ge(pe_gT, N(call, c12.k))
                    act.wait_ge(pe_w2, N(call, c12.k - 1))
                    copy(gT[:].rearrange("p c n -> p (c n)"), B3[:, 0:3 * P]).then_inc(ac_gT, 1)
                if a2.live:
                    act.wait_ge(dv_sm, N(call, a2.k))
                    for e in range(2):
                        for j in range(4):
                            m = act.activation(S[:, a2.par, e, j, :], S[:, a2.par, e, j, :], ACT.Exp,
                                               bias=nmx[:, a2.par, 4 * e + j:4 * e + j + 1])
                        m.then_inc(ac_P, 1)

            def rec_in(q, u):
                act.wait_ge(dv_y, SEQS * TPS + TILES + TPS * q + TPS)
                act.wait_ge(pe_lr_nT, due(q - 1))
                y = ys[:, q] if isinstance(q, int) else ys[:, bass.ds(q, 1)].rearrange("p a t d -> p (a t) d")
                copy(R_in[u].rearrange("p (t d) -> p t d", t=TPS), y).then_inc(ac_lr_in, 1)

            def rec_nT(q, u):
                act.wait_ge(pe_lr_nT, q + 1)
                act.wait_ge(po_lr_nx, due(q - 1))
                copy(R_nT[u], (B2, B3)[u][:]).then_inc(ac_lr_nT, 1)

            def rec_gates(q, u):
                act.wait_ge(pe_lr_g, q + 1)
                act.wait_ge(dv_lr_w, due(q - 1))
                gbank = (B01, B45)[u]
                act.activation(R_gx[u], gbank[:, 0:TOKENS], ACT.Sigmoid, bias=gate_b[:, 0:1])
                act.activation(R_ga[u], gbank[:, TOKENS:2 * TOKENS], ACT.Sigmoid, bias=gate_b[:, 1:2])\
                    .then_inc(ac_lr_g, 1)
                act.wait_ge(ac_lr_g, q + 1)
                act.wait_ge(dv_lr_p, due(q - 1))
                act.activation(R_a[u], R_ga[u], ACT.Exp, scale=decay[:, 0:1])
                act.wait_ge(ac_lr_m, due(q - 1))
                act.activation(R_a2[u], R_ga[u], ACT.Exp, scale=decay[:, 1:2]).then_inc(ac_lr_a, 1)
                act.wait_ge(dv_lr_m, q + 1)
                act.wait_ge(po_lr_nm, due(q - 1))
                act.activation(R_mult[u], R_a2[u], ACT.Sqrt, scale=-1.0).then_inc(ac_lr_m, 1)

            barrier(act, 1)
            pipeline(act, slot, 0)
            barrier(act, 2)
            rec_in(0, 0)
            rec_in(1, 1)
            rec_nT(0, 0)

            def step(q, u):
                if within(q, 0, SEQS - 2):
                    rec_nT(q + 1, 1 - u)
                rec_gates(q, u)
                if within(q, 0, SEQS - 3):
                    rec_in(q + 2, u)

            recurrence(act, step)
            barrier(act, 3)
            pipeline(act, slot, 1)

        @block.gpsimd
        def _(pool):
            def inverse_std(n, u):
                pool.wait_ge(dv_pst, n + 1)
                pool.tensor_tensor(prs[:, u], pmv[:, u, :, 1], half_neg[:, 0:TPS], ALU.pow).then_inc(po_prs, 1)

            def prepass(first):
                with pool.Fori(0, SEQS // 2) as i:
                    inverse_std(first + 2 * i, 0)
                    inverse_std(first + 2 * i + 1, 1)

            def slot(call, it, t, steady, at):
                g, nxt = at(0), at(-1)
                if nxt.live:
                    pool.wait_ge(dv_y, YCALL * call + nxt.k + 1)
                    pool.wait_ge(pe_yT, N(call, nxt.k - 2))
                    pool.tensor_copy(yst[:, nxt.par, :], tile_of(ys, nxt)).then_inc(po_y, 1)
                if g.live:
                    k = g.k
                    pool.wait_ge(po_q, N(call, k - 2))
                    pool.wait_ge(dv_ss, N(call, k))
                    pool.tensor_tensor(rn[:, g.par], ss[:, g.par], half_neg[:], ALU.pow).then_inc(po_rn, 1)
                    pool.wait_ge(dv_rope, N(call, k))
                    c4 = rot[:, g.par].rearrange("p (h f d) -> p h f d", f=2, d=DH // 2)
                    s4 = rsin[:, g.par].rearrange("p (h f d) -> p h f d", f=2, d=DH // 2)
                    pool.tensor_tensor(c4, c4, s4[:, :, 1::-1, :], ALU.add).then_inc(po_add, 1)
                    pool.wait_ge(po_add, N(call, k))
                    pool.wait_ge(po_rn, N(call, k))
                    c3 = rot[:, g.par].rearrange("p (h d) -> p h d", d=DH)
                    pool.tensor_tensor(c3, c3, rn[:, g.par].unsqueeze(2).broadcast_to([P, 2 * HEADS, DH]), ALU.mult)\
                        .then_inc(po_q, 1)
                if t == 0 and seq_live(it):
                    j = it - 2
                    pool.wait_ge(dv_ag, J(call, j))
                    pool.tensor_tensor(mr[:, 0:TPS, 1], mv[:, :, 1], half_neg[:, 0:TPS], ALU.pow).then_inc(po_rs, 1)

            def rec_products(q, u):
                pool.wait_ge(ac_lr_g, q + 1)
                pool.tensor_tensor(R_gx[u], R_gx[u], R_nT[u], ALU.mult).then_inc(po_lr_nx, 1)
                pool.wait_ge(po_lr_nx, q + 1)
                pool.wait_ge(ac_lr_m, q + 1)
                pool.tensor_tensor(R_gx[u], R_gx[u], R_mult[u], ALU.mult).then_inc(po_lr_nm, 1)

            pool.wait_ge(set_v, 1)
            prepass(0)
            pool.wait_ge(set_d, 4)
            pool.tensor_tensor(decay[:, 4:5], decay[:, 3:4], decay[:, 2:3], ALU.pow).then_inc(set_p, 1)
            barrier(pool, 1)
            pipeline(pool, slot, 0)
            barrier(pool, 2)
            for q in range(AHEAD + 1):
                inverse_std(SEQS + q, q % 2)

            def step(q, u):
                rec_products(q, u)
                if within(q, 0, SEQS - 2 - AHEAD):
                    inverse_std(SEQS + AHEAD + 1 + q, 1 - u)

            recurrence(pool, step)
            barrier(pool, 3)
            prepass(2 * SEQS)
            pipeline(pool, slot, 1)

        @block.vector
        def _(dve):
            links = [0]

            def link(ins):
                links[0] += 1
                ins.then_inc(set_d, 1)
                dve.wait_ge(set_d, links[0])

            def norm_stats(first, q, u):
                for t in range(TPS):
                    m = dve.bn_stats(pst[:, u, t, :], seq_tile(xs, q, t))
                m.then_inc(dv_pa, 1)
                dve.wait_ge(dv_pa, first + q + 1)
                settle(dve)
                for t in range(TPS):
                    m = dve.bn_aggr(pmv[:, u, t, :], pst[:, u, t, :])
                m.then_inc(dv_pag, 1)
                dve.wait_ge(dv_pag, first + q + 1)
                dve.tensor_scalar(pmv[:, u, :, 1], pmv[:, u, :, 1], EPS, None, ALU.add).then_inc(dv_pst, 1)

            def norm_apply(first, q, u):
                dve.wait_ge(po_prs, first + q + 1)
                for t in range(TPS):
                    dve.tensor_scalar(seq_tile(ys, q, t), seq_tile(xs, q, t), pmv[:, u, t, 0:1],
                                      prs[:, u, t:t + 1], ALU.subtract, ALU.mult).then_inc(dv_y, 1)

            def prepass(first):
                norm_stats(first, 0, 0)
                norm_stats(first, 1, 1)
                norm_apply(first, 0, 0)
                with dve.Fori(1, SEQS // 2) as i:
                    norm_stats(first, 2 * i, 0)
                    norm_apply(first, 2 * i - 1, 1)
                    norm_stats(first, 2 * i + 1, 1)
                    norm_apply(first, 2 * i, 0)
                norm_apply(first, SEQS - 1, 1)

            def setup():
                dve.memset(w2[:, :, 2, :], 0.0)
                dve.memset(gate_w[:], 0.0)
                dve.memset(b1s[:], 0.0)
                dve.memset(b2s[:], 0.0)
                dve.memset(ones_bf[:], 1.0)
                dve.memset(hT[:], 0.0)
                dve.memset(mT[:], 0.0)
                dve.memset(KT[:], 0.0)
                for v in (Vb, Va):
                    dve.memset(v[:, :, :, 0:DH], 0.0)
                    dve.memset(v[:, :, :, DH:DH + 1], 1.0)
                dve.memset(gg[:], 0.0)
                dve.memset(mr[:], 0.0)
                dve.memset(half_neg[:], -0.5)
                dve.memset(decay[:, 3:4], float(np.e))
                for c, v in enumerate((32.0, 0.0, 0.0, 32.0, 0.0, 0.0)):
                    m = dve.memset(tupB[:, 0, c:c + 1], v)
                m.then_inc(set_v, 1)
                dve.wait_ge(load_x, 64)
                prepass(0)
                dve.wait_ge(load_w, W_ALL)
                dve.wait_ge(set_v, 1)
                link(dve.tensor_scalar(decay[:, 5:6], decay[:, 0:1], -1.0, None, ALU.mult))
                link(dve.tensor_tensor(decay[:, 2:3], decay[:, 0:1], decay[:, 5:6], ALU.min))
                for l in range(LAYERS):
                    v = rope[:, l].rearrange("p a t n d -> p (a t) (n d)")
                    link(dve.tensor_tensor(v, v, qk_scale[:, l:l + 1].rearrange("p a n d -> p a (n d)")
                                           .broadcast_to([P, 2 * TPS, 2 * DH]), ALU.mult))
                for l in range(LAYERS):
                    m = dve.tensor_copy(QT[:, 0, l, 0:3], lnp_w[:, l, 1:2].broadcast_to([P, 3]))
                m.then_inc(set_v, 1)
                dve.wait_ge(set_e, 1)

                def three_parts(dst, b, f, h):
                    n = b.shape[-1]
                    hb = h.bitcast(BF16)
                    for part in range(3):
                        link(dve.tensor_copy(hb[:, part * n:(part + 1) * n], b))
                        if part < 2:
                            link(dve.tensor_tensor(b, b, hb[:, part * n:(part + 1) * n], ALU.subtract))
                    link(dve.tensor_scalar(f, hb[:, 0:n], cst[0:3, C_IDENT:C_IDENT + 1], None, ALU.mult))
                    link(dve.scalar_tensor_tensor(out=f, in0=hb[:, n:2 * n], scalar=cst[0:3, C_IDENT + 1:C_IDENT + 2],
                                                  in1=f, op0=ALU.mult, op1=ALU.add))
                    link(dve.scalar_tensor_tensor(out=dst, in0=hb[:, 2 * n:3 * n],
                                                  scalar=cst[0:3, C_IDENT + 2:C_IDENT + 3],
                                                  in1=f, op0=ALU.mult, op1=ALU.add))

                for l in range(LAYERS):
                    link(dve.tensor_scalar(w1[:, l], w1[:, l], lnp_w[:, l, 0:1], None, ALU.mult))
                    b = sq[0:3, 0:2 * HID] if l == 0 else rot[0:3, 0, 0:2 * HID]
                    bv = b.rearrange("p (n c) -> p n c", n=2)
                    made = (B01 if l == 0 else B45)[0:3].rearrange("p (n c) -> p n c", n=2)[:, :, 0:HID]
                    link(dve.tensor_tensor(bv, made, bv, ALU.add))
                    three_parts(b1s[0:3, l], b, rot[0:3, 1, 0:2 * HID], S[0:3].rearrange("p a e j n -> p (a e j n)"))
                    three_parts(b2s[0:3, l], rsin[0:3, 0, l * DIM:(l + 1) * DIM], rot[0:3, 1, 0:DIM],
                                S[0:3].rearrange("p a e j n -> p (a e j n)"))
                dve.wait_ge(set_p, 1)
                z, w, sc, s2, p = (decay[:, n:n + 1] for n in (4, 5, 6, 7, 2))
                link(dve.tensor_scalar(w, z, 2.0, None, ALU.add))
                link(dve.reciprocal(w, w))
                link(dve.tensor_tensor(sc, z, w, ALU.mult))
                link(dve.tensor_tensor(s2, sc, sc, ALU.mult))
                link(dve.memset(p, 1.0 / 21))
                for n in range(19, 0, -2):
                    link(dve.tensor_scalar(p, p, s2, 1.0 / n, ALU.mult, ALU.add))
                link(dve.tensor_tensor(p, p, sc, ALU.mult))
                link(dve.tensor_scalar(w, decay[:, 0:1], 0.0, None, ALU.max))
                link(dve.scalar_tensor_tensor(out=w, in0=p, scalar=2.0, in1=w, op0=ALU.mult, op1=ALU.add))
                link(dve.tensor_scalar(decay[:, 0:1], w, -8.0, None, ALU.mult))
                link(dve.tensor_scalar(decay[:, 1:2], w, -16.0, None, ALU.mult))
                dve.sem_inc(set_v, 1)

            def slot(call, it, t, steady, at):
                g, a1, a2, a3, a4 = (at(n) for n in range(5))
                nxt, c9, c10, c11, c12 = (at(n) for n in (-1, 9, 10, 11, 12))
                k = g.k
                if g.live:
                    dve.wait_ge(pe_kT, N(call, k - 2))
                    for n in range(2):
                        dve.wait_ge(ac_sq, N(call, k, 2, 1 + n))
                        q3 = B01[:, 512 * n:512 * (n + 1)].rearrange("p (h d) -> p h d", d=DH)
                        for cs, buf in enumerate((rot, rsin)):
                            m = dve.tensor_tensor(
                                buf[:, g.par, 512 * n:512 * (n + 1)].rearrange("p (h d) -> p h d", d=DH), q3,
                                rope_of(g, cs, n), ALU.mult)
                    m.then_inc(dv_rope, 1)
                if g.live:
                    dve.wait_ge(po_rn, N(call, k - 2))
                    dve.tensor_reduce(ss[:, g.par], sq[:].rearrange("p (h d) -> p h d", d=DH), AX.X, ALU.add)\
                        .then_inc(dv_sum, 1)
                    dve.wait_ge(dv_sum, N(call, k))
                    dve.tensor_scalar(ss[:, g.par], ss[:, g.par], 1e-24, None, ALU.max).then_inc(dv_ss, 1)
                if a2.live:
                    dve.wait_ge(pe_S, N(call, a2.k))
                    dve.wait_ge(pe_PT, N(call, a2.k - 2, 2, 2))
                    settle(dve)
                    mask = cst[:, C_MASK + (0 if a2.r == 0 else P):][:, 0:P]
                    for e in range(2):
                        for j in range(4):
                            h = 4 * e + j
                            m = dve.tensor_tensor_reduce(S[:, a2.par, e, j, :], B45[:, 512 * e + P * j:][:, 0:P], mask,
                                                         1.0, LOWEST, ALU.add, ALU.max, mx[:, a2.par, h:h + 1])
                    m.then_inc(dv_mx, 1)
                    dve.wait_ge(dv_mx, N(call, a2.k))
                    dve.tensor_scalar(nmx[:, a2.par], mx[:, a2.par], -1.0, None, ALU.mult).then_inc(dv_sm, 1)
                if c11.live:
                    dve.wait_ge(ac_gl, N(call, c11.k))
                    dve.wait_ge(pe_gT, N(call, c11.k - 2))
                    dve.tensor_tensor(gg[:, c11.par, 0:HID], B01[:, 0:HID], gl[:], ALU.mult).then_inc(dv_gg, 1)

                def divide(e):
                    dve.wait_ge(pe_O, N(call, a3.k, 2, 1 + e))
                    o3 = B7[:, 0:4 * (DH + 1)].rearrange("p (j d) -> p j d", d=DH + 1)
                    dve.reciprocal(rc[:], o3[:, :, DH]).then_inc(dv_rc, 1)
                    dve.wait_ge(dv_rc, N(call, a3.k, 2, 1 + e))
                    dve.wait_ge(pe_OT, N(call, a3.k - 2))
                    dve.tensor_tensor(O[:, a3.par].rearrange("p (j e d) -> p j e d", e=2, d=DH)[:, :, e, :],
                                      o3[:, :, 0:DH], rc[:].unsqueeze(2).broadcast_to([P, 4, DH]), ALU.mult)\
                        .then_inc(dv_O, 1)

                if a3.live:
                    divide(0)

                def shifted(dst, st, src):
                    c = P * st.r
                    dve.tensor_copy(dst[0:64, c:c + P], src[0:64, :])
                    return dve.tensor_copy(dst[64:128, c + 1:c + P + 1], src[64:128, :])

                if nxt.live:
                    dve.wait_ge(pe_yT, N(call, nxt.k))
                if c10.live:
                    dve.wait_ge(pe_nT, N(call, c10.k))
                if nxt.live:
                    shifted(hT, nxt, B2[:, 0:P]).then_inc(dv_hT, 1)
                if c10.live:
                    if c10.r == 0:
                        dve.tensor_copy(mT[64:128, 0:1], B2[64:128, 2 * P:2 * P + 1])
                    shifted(mT, c10, B2[:, P:2 * P]).then_inc(dv_mT, 1)
                if a3.live:
                    divide(1)
                if t == 0 and seq_live(it):
                    j = it - 2
                    dve.wait_ge(pe_st1, J(call, j))
                    dve.tensor_copy(tup[:, :, 6:12], B45[:, 0:TPS * 6].rearrange("p (t n) -> p t n", n=6))\
                        .then_inc(dv_tc, 1)
                    dve.wait_ge(dv_tc, J(call, j))
                    dve.wait_ge(dv_bn, N(call, TPS * j + TPS - 1))
                    dve.wait_ge(po_rs, J(call, j - 1))
                    settle(dve)
                    for r in range(TPS):
                        m = dve.bn_aggr(mv[:, r, :], tup[:, r, :])
                    m.then_inc(dv_agg, 1)
                    dve.wait_ge(dv_agg, J(call, j))
                    dve.tensor_scalar(mr[:, 0:TPS, 0], mv[:, :, 0], 0.0, None, ALU.add)
                    dve.tensor_scalar(mv[:, :, 1], mv[:, :, 1], EPS, None, ALU.add).then_inc(dv_ag, 1)
                if t == 1 and seq_live(it):
                    j = it - 2
                    dve.wait_ge(pe_st2, J(call, j))
                    dve.tensor_copy(lnp[:, :, 0, :], mr[:, 0:TPS, :])
                    dve.tensor_copy(lnp[:, :, 1, :], B45[:, 512:512 + 2 * TPS].rearrange("p (t n) -> p t n", n=2))\
                        .then_inc(dv_lp, 1)
                    dve.wait_ge(dv_lp, J(call, j))
                    dve.scalar_tensor_tensor(out=before[:], in0=lnp[:, 0, 0, 0:1].broadcast_to([P, 2]), scalar=-1.0,
                                             in1=lnp[:, 0, 0, 1:2].broadcast_to([P, 2]), op0=ALU.mult, op1=ALU.mult)
                if a4.live:
                    dve.wait_ge(pe_wo, N(call, a4.k))
                    y = tile_of(ys, a4)
                    dve.tensor_tensor(y, B6[:, 0:DIM], y, ALU.add).then_inc(dv_r1, 1)
                if c9.live:
                    dve.wait_ge(dv_lp, J(call, (c9.k - c9.r) // TPS if isinstance(c9.k, int) else it + c9.back))
                    dve.wait_ge(dv_r1, N(call, c9.k))
                    y = tile_of(ys, c9)
                    for f in range(2):
                        m = dve.tensor_scalar(nb[:, c9.r, 64 * f:64 * f + 64], y[:, 64 * f:64 * f + 64],
                                              lnp[:, c9.r, f, 0:1], lnp[:, c9.r, f, 1:2], ALU.subtract, ALU.mult)
                    m.then_inc(dv_ln, 1)
                if a4.live:
                    dve.wait_ge(dv_r1, N(call, a4.k))
                    settle(dve)
                    y = tile_of(ys, a4)
                    dve.bn_stats(tup[:, a4.r, 0:6], y[:, 0:64])
                    dve.bn_stats(tupB[:, a4.r + 1, :], y[:, 64:128]).then_inc(dv_bn, 1)
                if a1.live:
                    dve.wait_ge(ac_v, N(call, a1.k))
                    dve.wait_ge(pe_O, N(call, a1.k - 3, 2, 2))
                    dve.tensor_copy(Va[0:64, a1.r, :, 0:DH], Vb[0:64, a1.r, :, 0:DH])
                    dve.tensor_copy(Va[64:128, (a1.r + 1) % TPS, :, 0:DH], Vb[64:128, a1.r, :, 0:DH])\
                        .then_inc(dv_vc, 1)
                if c12.live:
                    dve.wait_ge(pe_w2, N(call, c12.k))
                    y = tile_of(ys, c12)
                    dve.tensor_tensor(y, B2[:, 0:DIM], y, ALU.add).then_inc(dv_y, 1)

            def block_residual(call):
                dve.wait_ge(dv_y, Y(call, TILES - 1))
                for q in range(4):
                    x = xs[:, 4 * q:4 * q + 4].rearrange("p s t d -> p (s t d)")
                    y = ys[:, 4 * q:4 * q + 4].rearrange("p s t d -> p (s t d)")
                    dve.scalar_tensor_tensor(out=x, in0=y, scalar=0.5, in1=x, op0=ALU.mult, op1=ALU.add)\
                        .then_inc(dv_x, 1)

            def rec_clip(q, u):
                dve.wait_ge(ac_lr_a, q + 1)
                dve.tensor_scalar(R_a2[u], R_a2[u], 1.0, -1e-7, ALU.subtract, ALU.min).then_inc(dv_lr_m, 1)

            def rec_scan(q, u):
                zero = zero_col[:].broadcast_to([P, TOKENS])
                dve.tensor_tensor_scan(R_p[u][:, 1:TOKENS + 1], R_a[u], zero, 1.0, ALU.mult, ALU.add)\
                    .then_inc(dv_lr_p, 1)
                dve.wait_ge(dv_lr_p, q + 1)
                dve.tensor_scalar(R_pc[u], R_p[u][:, 0:TOKENS], 1e-7, None, ALU.max).then_inc(dv_lr_pc, 1)
                dve.wait_ge(dv_lr_pc, q + 1)
                dve.reciprocal(R_rec[u], R_pc[u]).then_inc(dv_lr_rec, 1)
                dve.wait_ge(dv_lr_rec, q + 1)
                dve.wait_ge(po_lr_nm, q + 1)
                dve.wait_ge(pe_lr_h, due(q - 1))
                dve.tensor_tensor(R_w[u], R_gx[u], R_rec[u], ALU.mult).then_inc(dv_lr_w, 1)
                dve.wait_ge(dv_lr_w, q + 1)
                dve.tensor_tensor_scan(R_S[u], R_w[u], zero, 0.0, ALU.add, ALU.add).then_inc(dv_lr_S, 1)
                dve.wait_ge(dv_lr_S, q + 1)
                dve.tensor_tensor(R_w[u], R_pc[u], R_S[u], ALU.mult).then_inc(dv_lr_h, 1)

            def rec_add(q, u):
                dve.wait_ge(pe_lr_h, q + 1)
                x = xs[:, q] if isinstance(q, int) else xs[:, bass.ds(q, 1)].rearrange("p a t d -> p (a t) d")
                dve.tensor_tensor(x, (B6, B7)[u][:].rearrange("p (t d) -> p t d", t=TPS), x, ALU.add)\
                    .then_inc(dv_lr_x, 1)

            setup()
            barrier(dve, 1)
            pipeline(dve, slot, 0)
            block_residual(0)
            barrier(dve, 2)
            dve.wait_ge(dv_x, 4)
            for u in turns:
                dve.memset(R_p[u][:, 0:1], 1.0)
            dve.memset(zero_col[:], 0.0).then_inc(dv_z, 1)
            dve.wait_ge(dv_z, 1)
            norm_stats(SEQS, 0, 0)
            for q in range(AHEAD):
                norm_stats(SEQS, q + 1, (q + 1) % 2)
                norm_apply(SEQS, q, q % 2)
            rec_clip(0, 0)

            def step(q, u):
                if within(q, 0, SEQS - 2):
                    rec_clip(q + 1, 1 - u)
                rec_scan(q, u)
                if within(q, 0, SEQS - 2 - AHEAD):
                    norm_stats(SEQS, q + AHEAD + 1, 1 - u)
                if within(q, 0, SEQS - 1 - AHEAD):
                    norm_apply(SEQS, q + AHEAD, u)
                if within(q, 1, SEQS - 1):
                    rec_add(q - 1, 1 - u)

            recurrence(dve, step)
            rec_add(SEQS - 1, 1)
            barrier(dve, 3)
            dve.wait_ge(dv_lr_x, SEQS)
            prepass(2 * SEQS)
            pipeline(dve, slot, 1)
            block_residual(1)


_INS = ["L0_attn_x", "L0_attn_ig_w", "L0_attn_ig_b", "L0_attn_ag_w", "L0_attn_ag_b", "L0_attn_a_param", "L0_ffn_wqkv",
        "L0_ffn_q_scale", "L0_ffn_k_scale", "L0_ffn_wo", "L0_ffn_ln_g", "L0_ffn_ln_b", "L0_ffn_w1", "L0_ffn_b1",
        "L0_ffn_w2", "L0_ffn_b2"]


def kernel(**inputs):
    import numpy as _np
    import concourse.bacc as _bacc
    from concourse import mybir as _mybir
    from concourse.bass_utils import run_bass_kernel_spmd as _run

    nc = _bacc.Bacc("TRN2", target_bir_lowering=False, num_devices=1)
    arrays, args = {}, []
    for name in _INS:
        arrays[f"in_{name}"] = _np.ascontiguousarray(inputs[name])
    arrays["in_consts"] = shape_constants()
    for name, a in arrays.items():
        args.append(nc.dram_tensor(name, a.shape, _mybir.dt.from_np(a.dtype), kind="ExternalInput").ap())
    args.append(nc.dram_tensor("out_0", (SEQS, TOKENS, DIM), _mybir.dt.float32, kind="ExternalOutput").ap())
    build(nc, *args)
    r = _run(nc, [arrays], core_ids=[0])
    return r.results[0]["out_0"]
```

```python
from contextlib import ExitStack
from itertools import count

import numpy as np

import concourse.bass as bass
from concourse import mybir

F32 = mybir.dt.float32
BF16 = mybir.dt.bfloat16
F32R = mybir.dt.float32r
ALU = mybir.AluOpType
ACT = mybir.ActivationFunctionType
AX = mybir.AxisListType

P = 128
SEQS, TOKENS, DIM = 16, 512, 128
TPS = TOKENS // P
HEADS, DH, WINDOW = 8, 64, 64
INNER = HEADS * DH
HID = int(DIM * 4 * 2 / 3)
HIDP = 3 * P
LAYERS = 2
TILES = LAYERS * SEQS * TPS
ITERS = LAYERS * SEQS
FILL = 4
DRAIN = 3
YCALL = 2 * SEQS * TPS + TILES
BLOCKS = 8
AHEAD = 4
QK_SCALE = 8.0
EPS = 1e-5
MASKED = -1e30
LOWEST = -3.0e38

C_IDENT, C_DOWN, C_FROM_PREV, C_UP, C_FROM_NEXT, C_MASK, C_FIRST, C_ROPE = (
    0, 128, 256, 384, 512, 640, 896, 1024)
C_ALL = C_ROPE + 2 * TPS * 2 * DH


def shape_constants():
    c = np.zeros((P, C_ALL), np.float32)
    i = np.arange(P)
    c[i, C_IDENT + i] = 1.0
    c[i[:-1], C_DOWN + i[1:]] = 1.0
    c[P - 1, C_FROM_PREV] = 1.0
    c[i[1:], C_UP + i[:-1]] = 1.0
    c[0, C_FROM_NEXT + P - 1] = 1.0
    c[0, C_FIRST:C_FIRST + P] = 1.0
    qi = np.arange(WINDOW)[:, None]
    kj = np.arange(WINDOW)[None, :]
    own, prev = np.where(kj <= qi, 0.0, MASKED), np.where(kj >= qi, 0.0, MASKED)
    odd_rows = np.concatenate([prev, own], axis=1)
    first = np.concatenate([np.concatenate([own, np.full_like(prev, MASKED)], 1), odd_rows], 0)
    other = np.concatenate([np.concatenate([own, prev], 1), odd_rows], 0)
    c[:, C_MASK:C_MASK + P], c[:, C_MASK + P:C_MASK + 2 * P] = first, other
    half = np.arange(0, DH, 2, dtype=np.float32)
    inv = (np.float32(1.0) / np.float32(10000.0) ** (half / np.float32(DH))).astype(np.float32)
    pos = np.arange(TOKENS, dtype=np.float32)
    ang = (pos[:, None] * inv[None, :]).astype(np.float32).astype(np.float64)
    base = ((half + np.float32(0.4 * DH)) / np.float32(1.4 * DH)).astype(np.float64)
    scale = base[None, :] ** ((pos - TOKENS // 2) / float(WINDOW // 2))[:, None]
    cos, sin = np.cos(ang), np.sin(ang)
    rope = np.zeros((TOKENS, 2, 2, DH))
    for n, s in enumerate((scale * QK_SCALE, 1.0 / scale)):
        rope[:, 0, n] = np.concatenate([cos * s, cos * s], -1)
        rope[:, 1, n] = np.concatenate([sin * s, -sin * s], -1)
    rope = rope.reshape(TPS, P, 2, 2, DH).transpose(1, 2, 0, 3, 4)
    c[:, C_ROPE:] = rope.reshape(P, -1)
    return c


class Stage:

    def __init__(self, it, t, lag, regs):
        d = t - lag
        self.r, self.back = d % TPS, d // TPS
        self.k = TPS * (it + self.back) + self.r
        self.live = not isinstance(self.k, int) or 0 <= self.k < TILES
        if self.live:
            self.seq, self.layer = regs(self.back)
        self.par = self.r % 2


def due(value):
    return max(value, 0) if isinstance(value, int) else value


def build(nc, x_in, ig_w, ig_b, ag_w, ag_b, a_param, wqkv_in, q_scale, k_scale, wo_in, ln_g, ln_b, w1_in, b1_in,
          w2_in, b2_in, consts, out):
    with ExitStack() as ctx:
        def sb(name, shape, dt=F32):
            return ctx.enter_context(nc.sbuf_tensor(name, shape, dt))

        def ps(name, cols):
            return ctx.enter_context(nc.psum_tensor(name, [P, cols], F32))

        def sem(name):
            return ctx.enter_context(nc.semaphore(name))

        xs = sb("xs", [P, SEQS, TPS, DIM])
        ys = sb("ys", [P, SEQS, TPS, DIM])
        wqkv_hi = sb("wqkv_hi", [P, LAYERS, 3 * INNER], F32R)
        wqkv_lo = sb("wqkv_lo", [P, LAYERS, 3 * INNER], F32R)
        wo = sb("wo", [P, LAYERS, INNER // P, DIM])
        w1 = sb("w1", [P, LAYERS, 2 * HID])
        w2 = sb("w2", [P, LAYERS, 3, DIM])
        b1s = sb("b1s", [P, LAYERS, 2 * HID], BF16)
        b2s = sb("b2s", [P, LAYERS, DIM], BF16)
        ones_bf = sb("ones_bf", [P, P], BF16)
        cst = sb("cst", [P, C_ROPE])
        rope = sb("rope", [P, LAYERS, 2, TPS, 2, DH])
        gate_w = sb("gate_w", [P, 2, DIM])
        gate_b = sb("gate_b", [P, 2])
        decay = sb("decay", [P, 8])
        lnp_w = sb("lnp_w", [P, LAYERS, 2])
        qk_scale = sb("qk_scale", [P, LAYERS, 2, DH])
        scratch = sb("scratch", [P, 8])
        table_scratch = sb("table_scratch", [P, 8])
        zero_col = sb("zero_col", [P, 1])
        half_neg = sb("half_neg", [P, 16])
        yst = sb("yst", [P, 2, DIM])
        hT = sb("hT", [P, TOKENS + 1], F32R)
        hT_lo = sb("hT_lo", [P, TOKENS + 1], F32R)
        mT = sb("mT", [P, TOKENS + 1])
        sq = sb("sq", [P, 2 * INNER])
        rot = sb("rot", [P, 2, 2 * INNER])
        rsin = sb("rsin", [P, 2, 2 * INNER])
        ss = sb("ss", [P, 2, 2 * HEADS])
        rn = sb("rn", [P, 2, 2 * HEADS])
        QT = sb("QT", [P, 4, TPS, P])
        KT = sb("KT", [P, 4, TPS, P])
        Vb = sb("Vb", [P, TPS, HEADS, DH])
        Va = sb("Va", [P, TPS, HEADS, DH])
        S = sb("S", [P, 2, 2, 4, P])
        mx = sb("mx", [P, 2, 8])
        nmx = sb("nmx", [P, 2, 8])
        PT = sb("PT", [P, 2, 4, P])
        rsum = sb("rsum", [P, 2, 8])
        rinv = sb("rinv", [P, 2, 8])
        OT = sb("OT", [P, 2, 4, P])
        tup = sb("tup", [P, TPS, 12])
        tupB = sb("tupB", [P, TPS + 1, 6])
        mv = sb("mv", [P, TPS, 2])
        mr = sb("mr", [P, TPS + 1, 2])
        lnp = sb("lnp", [P, TPS, 2, 2])
        before = sb("before", [P, 2])
        nb = sb("nb", [P, TPS, DIM])
        gl = sb("gl", [P, HID])
        gg = sb("gg", [P, 2, HIDP])
        gT = sb("gT", [P, 3, P])
        pst = sb("pst", [P, 2, TPS, 6])
        pmv = sb("pmv", [P, 2, TPS, 2])
        prs = sb("prs", [P, 2, TPS])

        ident = cst[:, C_IDENT:C_IDENT + P]
        down, from_prev = cst[:, C_DOWN:C_DOWN + P], cst[:, C_FROM_PREV:C_FROM_PREV + P]
        first_row = cst[:, C_FIRST:C_FIRST + P]
        up, from_next = cst[:, C_UP:C_UP + P], cst[:, C_FROM_NEXT:C_FROM_NEXT + P]

        B01, B2, B3 = ps("B01", 1024), ps("B2", 512), ps("B3", 512)
        B45, B6, B7 = ps("B45", 1024), ps("B6", 512), ps("B7", 512)

        turns = range(2)
        R_in = [sq[:, 512 * u:512 * (u + 1)] for u in turns]
        R_nT, R_gx = [rot[:, u, 0:512] for u in turns], [rot[:, u, 512:1024] for u in turns]
        R_ga, R_a = [rsin[:, u, 0:512] for u in turns], [rsin[:, u, 512:1024] for u in turns]
        R_a2, R_mult = ([S[:, u, e].rearrange("p j n -> p (j n)") for u in turns] for e in range(2))
        w_in = [buf[:].rearrange("p c t n -> p (c t n)")[:, 0:3 * INNER] for buf in (QT, KT)]
        QTf, KTf = QT[:].rearrange("p c t n -> p (c t n)"), KT[:].rearrange("p c t n -> p (c t n)")
        R_p = [QTf[:, 1024 * u:1024 * u + TOKENS + 1] for u in turns]
        R_pc = [KTf[:, 1024 * u:1024 * u + 512] for u in turns]
        R_rec = [KTf[:, 1024 * u + 512:1024 * u + 1024] for u in turns]
        R_w, R_S = ([buf[:, u].rearrange("p j n -> p (j n)") for u in turns] for buf in (PT, OT))

        load_w, load_x, stored = sem("load_w"), sem("load_x"), sem("stored")
        set_v, set_p, set_e, set_d, phase = sem("set_v"), sem("set_p"), sem("set_e"), sem("set_d"), sem("phase")
        pe_qk, pe_v, pe_qT, pe_kT = sem("pe_qk"), sem("pe_v"), sem("pe_qT"), sem("pe_kT")
        pe_S, pe_PT, pe_O = sem("pe_S"), sem("pe_PT"), sem("pe_O")
        pe_wo, pe_yT, pe_nT, pe_h = sem("pe_wo"), sem("pe_yT"), sem("pe_nT"), sem("pe_h")
        pe_gT, pe_w2, pe_st1, pe_st2 = sem("pe_gT"), sem("pe_w2"), sem("pe_st1"), sem("pe_st2")
        pe_lr_nT, pe_lr_g, pe_lr_h = sem("pe_lr_nT"), sem("pe_lr_g"), sem("pe_lr_h")
        dv_y, dv_rope, dv_ss, dv_vc = sem("dv_y"), sem("dv_rope"), sem("dv_ss"), sem("dv_vc")
        dv_mx, dv_sm, dv_rinv = sem("dv_mx"), sem("dv_sm"), sem("dv_rinv")
        dv_hT, dv_mT, dv_gg, dv_r1 = sem("dv_hT"), sem("dv_mT"), sem("dv_gg"), sem("dv_r1")
        dv_bn, dv_ln, dv_tc, dv_ag = sem("dv_bn"), sem("dv_ln"), sem("dv_tc"), sem("dv_ag")
        dv_hh, dv_lp, dv_agg, dv_pag, dv_sum = sem("dv_hh"), sem("dv_lp"), sem("dv_agg"), sem("dv_pag"), sem("dv_sum")
        dv_pa, dv_pst, dv_x, dv_z = sem("dv_pa"), sem("dv_pst"), sem("dv_x"), sem("dv_z")
        dv_lr_m, dv_lr_p, dv_lr_pc, dv_lr_rec = sem("dv_lr_m"), sem("dv_lr_p"), sem("dv_lr_pc"), sem("dv_lr_rec")
        dv_lr_w, dv_lr_S, dv_lr_h, dv_lr_x = sem("dv_lr_w"), sem("dv_lr_S"), sem("dv_lr_h"), sem("dv_lr_x")
        ac_sq, ac_v, ac_qT, ac_kT = sem("ac_sq"), sem("ac_v"), sem("ac_qT"), sem("ac_kT")
        ac_P, ac_PT, ac_gl, ac_OT = sem("ac_P"), sem("ac_PT"), sem("ac_gl"), sem("ac_OT")
        ac_gT, ac_lr_in, ac_lr_nT, ac_lr_g = sem("ac_gT"), sem("ac_lr_in"), sem("ac_lr_nT"), sem("ac_lr_g")
        ac_lr_a, ac_lr_m = sem("ac_lr_a"), sem("ac_lr_m")
        po_rn, po_add, po_q, po_rs, po_P = sem("po_rn"), sem("po_add"), sem("po_q"), sem("po_rs"), sem("po_P")
        po_prs, po_y, po_lr_nx, po_lr_nm = sem("po_prs"), sem("po_y"), sem("po_lr_nx"), sem("po_lr_nm")

        def N(call, k, per=1, j=1):
            if isinstance(k, int):
                k = min(k, TILES - 1)
            return due(per * (TILES * call + k) + j)

        def Y(call, k):
            if isinstance(k, int):
                k = min(k, TILES - 1)
            return due(YCALL * call + SEQS * TPS + k + 1)

        def seq_live(it):
            return not isinstance(it, int) or 0 <= it - 2 < ITERS

        def J(call, j):
            return due(ITERS * call + j + 1)

        def barrier(eng, n):
            eng.drain().then_inc(phase, 1)
            eng.wait_ge(phase, 4 * n)

        scratch_turn = count()

        def settle(eng):
            if eng is nc.tensor:
                eng.matmul(B45[:, 0:64], ones_bf[:], ones_bf[:, 0:64], start=True, stop=True)
            else:
                n = next(scratch_turn) % 8
                eng.memset(scratch[:, n:n + 1], 0.0)

        def wo_out(t):
            return B45[:, 0:DIM] if t == 1 else B45[:, 512:512 + DIM]

        def tile_of(buf, st):
            if isinstance(st.seq, int):
                return buf[:, st.seq, st.r, :]
            return buf[:, bass.ds(st.seq, 1), st.r, :].rearrange("p a d -> p (a d)")

        def seq_tile(buf, q, t):
            if isinstance(q, int):
                return buf[:, q, t, :]
            return buf[:, bass.ds(q, 1), t, :].rearrange("p a d -> p (a d)")

        def of_layer(buf, st, a, b):
            n = len(buf.shape)
            flat = buf[:] if n == 3 else buf[:].rearrange("p l c d -> p l (c d)")
            if isinstance(st.layer, int):
                return flat[:, st.layer, a:b]
            return flat[:, bass.ds(st.layer, 1), a:b].rearrange("p a d -> p (a d)")

        def rope_of(st, cs, n):
            if isinstance(st.layer, int):
                v = rope[:, st.layer, cs, st.r, n, :].unsqueeze(1)
            else:
                v = rope[:, bass.ds(st.layer, 1), cs, st.r, n, :]
            return v.broadcast_to([P, HEADS, DH])

        def pipeline(eng, slot, call):
            def regs_at(it):
                kept = {}

                def regs(back):
                    if isinstance(it, int):
                        return (it + back) % SEQS, (it + back) // SEQS
                    if back not in kept:
                        kept[back] = (eng.snap((it + back) % SEQS), eng.snap((it + back) // SEQS))
                    return kept[back]
                return regs

            def iteration(it, steady):
                regs = regs_at(it)
                for t in range(TPS):
                    slot(call, it, t, steady, lambda lag: Stage(it, t, lag, regs))

            slot(call, -1, TPS - 1, False, lambda lag: Stage(-1, TPS - 1, lag, regs_at(-1)))
            for it in range(FILL):
                iteration(it, False)
            with eng.Fori(FILL, ITERS - 1) as it:
                iteration(it, True)
            for it in range(ITERS - 1, ITERS + DRAIN):
                iteration(it, False)

        def recurrence(eng, step):
            for q in range(4):
                step(q, q % 2)
            with eng.Fori(2, 5) as i:
                step(2 * i, 0)
                step(2 * i + 1, 1)
            for q in range(10, SEQS):
                step(q, q % 2)

        def within(q, first, last):
            return not isinstance(q, int) or first <= q <= last

        block = ctx.enter_context(nc.Block())
        x_t = x_in.rearrange("s (t p) d -> p s t d", p=P)
        o_t = out.rearrange("s (t p) d -> p s t d", p=P)
        n_weights = []

        @block.sync
        def _(sp):
            def load(dst, src):
                sp.dma_start(dst, src).then_inc(load_w, 16)
                n_weights.append(1)
            for q in range(4):
                sp.dma_start(xs[:, 4 * q:4 * q + 4].rearrange("p s t d -> p (s t) d"),
                             x_t[:, 4 * q:4 * q + 4].rearrange("p s t d -> p (s t) d")).then_inc(load_x, 16)
            load(cst[:], consts[:, 0:C_ROPE])
            for l in range(LAYERS):
                load(rope[:, l].rearrange("p a t n d -> p (a t n d)"), consts[:, C_ROPE:C_ALL])
                load(w_in[l], wqkv_in[l])
                load(wo[:, l], wo_in[l].rearrange("(c p) d -> p c d", p=P))
                load(w1[:, l], w1_in[l])
                load(w2[:, l, 0:2], w2_in[l, 0:2 * P].rearrange("(c p) d -> p c d", p=P))
                load(lnp_w[:, l, 0:1], ln_g[l:l + 1].rearrange("a d -> d a"))
                load(lnp_w[:, l, 1:2], ln_b[l:l + 1].rearrange("a d -> d a"))
                load(qk_scale[:, l, 0], q_scale[l:l + 1].broadcast_to([P, DH]))
                load(qk_scale[:, l, 1], k_scale[l:l + 1].broadcast_to([P, DH]))
                load(sq[0:3, 0:2 * HID] if l == 0 else rot[0:3, 0, 0:2 * HID],
                     b1_in[l:l + 1].broadcast_to([3, 2 * HID]))
                load(rsin[0:3, 0, l * DIM:(l + 1) * DIM], b2_in[l:l + 1].broadcast_to([3, DIM]))
            sp.wait_ge(set_v, 1)
            for l in range(LAYERS):
                load(w2[0:HID - 2 * P, l, 2], w2_in[l, 2 * P:HID])
            bw = DIM // BLOCKS
            for n, (w, b) in enumerate(((ig_w, ig_b), (ag_w, ag_b))):
                for i in range(BLOCKS):
                    load(gate_w[i * bw:(i + 1) * bw, n, i * bw:(i + 1) * bw], w[i])
                load(gate_b[:, n:n + 1], b.rearrange("h (i a) -> (h i) a", a=1))
            load(decay[:, 0:1], a_param.rearrange("(d a) -> d a", a=1))
            for q in range(4):
                sp.wait_ge(dv_x, 4 + q + 1)
                sp.dma_start(o_t[:, 4 * q:4 * q + 4].rearrange("p s t d -> p (s t) d"),
                             xs[:, 4 * q:4 * q + 4].rearrange("p s t d -> p (s t) d")).then_inc(stored, 16)
            sp.wait_ge(stored, 64)

        W_ALL = 16 * len(n_weights)

        @block.tensor
        def _(pe):
            pe.wait_ge(load_w, W_ALL)
            pe.wait_ge(set_v, 2)
            for l in range(LAYERS):
                for n in range(2):
                    m = pe.matmul(B01[0:3, 512 * n:512 * n + HID] if l == 0 else B45[0:3, 512 * n:512 * n + HID],
                                  PT[:, 0, l, 0:3], w1[:, l, n * HID:(n + 1) * HID], start=True, stop=True)
            m.then_inc(set_e, 1)
            pe.wait_ge(set_v, 3)

            def slot(call, it, t, steady, at):
                g, a1, a2, a3, a4 = at(0), at(1), at(2), at(3), at(4)
                nxt, c10, c11, c12 = at(-1), at(10), at(11), at(12)
                k = g.k
                if g.live:
                    pe.wait_ge(dv_gg, N(call, k - 12))
                    if not steady:
                        pe.wait_ge(dv_rope, N(call, k - 1, 2, 2))
                        pe.wait_ge(ac_sq, N(call, k - 1, 2, 2))
                    pe.wait_ge(dv_hT, N(call, k))
                    cols = slice(P * g.r, P * (g.r + 1))

                    def times_w(o, n):
                        hi, lo = (of_layer(w, g, INNER * n, INNER * (n + 1)) for w in (wqkv_hi, wqkv_lo))
                        pe.matmul(o, hT[:, cols], hi, start=True, stop=False)
                        pe.matmul(o, hT_lo[:, cols], hi, start=False, stop=False)
                        return pe.matmul(o, hT[:, cols], lo, start=False, stop=True)

                    for n in range(2):
                        m = times_w(B01[:, 512 * n:512 * (n + 1)], n)
                    m.then_inc(pe_qk, 1)
                    pe.wait_ge(dv_y, Y(call, k - 13))
                    if not steady:
                        pe.wait_ge(dv_mT, N(call, k - 11))
                    times_w(B2[:, :], 2).then_inc(pe_v, 1)
                if a1.live:
                    pe.wait_ge(po_q, N(call, a1.k))
                    pe.wait_ge(ac_gT, N(call, k - 13))
                    if not steady:
                        pe.wait_ge(ac_kT, N(call, k - 2))
                    for c in range(4):
                        m = pe.transpose(B3[:, P * c:P * (c + 1)], rot[:, a1.par, P * c:P * (c + 1)], ident)
                    m.then_inc(pe_qT, 1)
                if a2.live:
                    pe.wait_ge(ac_qT, N(call, a2.k))
                    pe.wait_ge(ac_kT, N(call, a2.k))
                    pe.wait_ge(dv_sm, N(call, a2.k - 1))
                    pe.wait_ge(dv_r1, N(call, k - 5))
                    if t == 1 and seq_live(it):
                        pe.wait_ge(dv_tc, J(call, it - 2))
                    if t == 2 and seq_live(it):
                        pe.wait_ge(dv_lp, J(call, it - 2))
                    settle(pe)
                    r = a2.r
                    for j in range(4):
                        for e in range(2):
                            rows = slice(64 * e, 64 * e + 64)
                            kh = KT[rows, j].rearrange("p t (w n) -> p (t w) n", n=WINDOW)
                            ka = kh[:, 0:8:7, :] if r == 0 else kh[:, 2 * r:(2 * r - 2 if r > 1 else 0):-1, :]
                            pe.matmul(B45[0:64, 512 * e + P * j:512 * e + P * (j + 1)], QT[rows, j, r, 0:64],
                                      ka, start=True, stop=True)
                            m = pe.matmul(B45[64:128, 512 * e + P * j:512 * e + P * (j + 1)], QT[rows, j, r, 64:128],
                                          KT[rows, j, r, :], start=True, stop=True)
                    m.then_inc(pe_S, 1)
                if a1.live:
                    pe.wait_ge(ac_qT, N(call, a1.k))
                    for c in range(4):
                        m = pe.transpose(B3[:, P * c:P * (c + 1)], rot[:, a1.par, INNER + P * c:INNER + P * (c + 1)],
                                         ident)
                    m.then_inc(pe_kT, 1)

                def probs_T(half):
                    pe.wait_ge(po_P, N(call, a3.k, 2, 1 + half))
                    pe.wait_ge(ac_PT, N(call, a3.k, 2, half))
                    for j in range(4):
                        m = pe.transpose(B6[:, P * j:P * (j + 1)], S[:, a3.par, half, j, :], ident)
                    m.then_inc(pe_PT, 1)

                def times_v(half):
                    pe.wait_ge(ac_PT, N(call, a3.k, 2, 1 + half))
                    if half == 0:
                        pe.wait_ge(ac_OT, N(call, a3.k - 1))
                        pe.wait_ge(dv_vc, N(call, a3.k))
                    for pair in range(2):
                        for w, v in enumerate((Va, Vb)):
                            for odd in range(2):
                                n, c = 2 * pair + odd, P * (2 * half + pair) + 64 * w
                                m = pe.matmul(B7[64 * odd:64 * odd + 64, c:c + 64], v[:, a3.r, 4 * half + n, :],
                                              PT[:, half, n, 64 * w:64 * w + 64], start=True, stop=True)
                    m.then_inc(pe_O, 1)

                if a3.live:
                    probs_T(0)
                if c11.live:
                    pe.wait_ge(dv_mT, N(call, c11.k))
                    pe.wait_ge(dv_rope, N(call, k, 2, 2))
                    pe.wait_ge(ac_sq, N(call, k, 2, 2))
                    if not steady:
                        pe.wait_ge(dv_gg, N(call, c11.k - 1))
                    for n in range(2):
                        o = B01[:, 512 * n:512 * n + HID]
                        pe.matmul(o, ones_bf[:], of_layer(b1s, c11, HID * n, HID * (n + 1)), start=True, stop=False)
                        m = pe.matmul(o, mT[:, P * c11.r:P * (c11.r + 1)], of_layer(w1, c11, HID * n, HID * (n + 1)),
                                      start=False, stop=True)
                    m.then_inc(pe_h, 1)
                if a3.live:
                    times_v(0)
                    probs_T(1)
                if nxt.live or c10.live:
                    pe.wait_ge(ac_v, N(call, k))
                    if not steady:
                        pe.wait_ge(dv_y, Y(call, k - 13))
                        pe.wait_ge(dv_mT, N(call, k - 11))
                if nxt.live:
                    pe.wait_ge(po_y, N(call, nxt.k))
                    pe.transpose(B2[:, 0:P], yst[:, nxt.par, :], ident).then_inc(pe_yT, 1)
                if c10.live:
                    pe.wait_ge(dv_ln, N(call, c10.k))
                    if c10.r == 0:
                        pe.matmul(B2[:, 2 * P:2 * P + 2], first_row, before[:], start=True, stop=True)
                    pe.transpose(B2[:, P:2 * P], nb[:, c10.r, :], ident).then_inc(pe_nT, 1)
                if c12.live:
                    pe.wait_ge(dv_gg, N(call, c12.k))
                    pe.wait_ge(ac_kT, N(call, k - 1))
                    if not steady:
                        pe.wait_ge(ac_gT, N(call, k - 13))
                    for c in range(3):
                        m = pe.transpose(B3[:, P * c:P * (c + 1)], gg[:, c12.par, P * c:P * (c + 1)], ident)
                    m.then_inc(pe_gT, 1)
                if a4.live:
                    pe.wait_ge(ac_OT, N(call, a4.k))
                    pe.wait_ge(dv_sm, N(call, k - 2))
                    if not steady:
                        pe.wait_ge(dv_r1, N(call, k - 5))
                        if t in (1, 2) and seq_live(it):
                            pe.wait_ge((dv_tc, dv_lp)[t - 1], J(call, it - 2))
                    o = wo_out(t)
                    for c in range(4):
                        m = pe.matmul(o, OT[:, a4.par, c, :], of_layer(wo, a4, DIM * c, DIM * (c + 1)),
                                      start=(c == 0), stop=(c == 3))
                    m.then_inc(pe_wo, 1)
                if a3.live:
                    times_v(1)
                if t == 0 and seq_live(it):
                    j = it - 2
                    pe.wait_ge(dv_bn, N(call, TPS * j + TPS - 1))
                    pe.wait_ge(dv_sm, N(call, a2.k))
                    o = B45[:, 0:TPS * 6]
                    pe.matmul(o, down, tupB[:, 1:TPS + 1, :].rearrange("p t n -> p (t n)"), start=True, stop=False)
                    pe.matmul(o, from_prev, tupB[:, 0:TPS, :].rearrange("p t n -> p (t n)"), start=False, stop=True)\
                        .then_inc(pe_st1, 1)
                if t == 1 and seq_live(it):
                    j = it - 2
                    pe.wait_ge(po_rs, J(call, j))
                    pe.wait_ge(dv_sm, N(call, a2.k))
                    if not steady:
                        pe.wait_ge(dv_r1, N(call, k - 5))
                    o = B45[:, 512:512 + TPS * 2]
                    pe.matmul(o, up, mr[:, 0:TPS, :].rearrange("p t n -> p (t n)"), start=True, stop=False)
                    pe.matmul(o, from_next, mr[:, 1:TPS + 1, :].rearrange("p t n -> p (t n)"), start=False, stop=True)\
                        .then_inc(pe_st2, 1)
                if c12.live:
                    pe.wait_ge(ac_gT, N(call, c12.k))
                    pe.wait_ge(dv_mT, N(call, k - 10))
                    pe.wait_ge(dv_hT, N(call, k + 1))
                    if not steady:
                        pe.wait_ge(ac_v, N(call, k))
                        pe.wait_ge(dv_y, Y(call, k - 13))
                    o = B2[:, 0:DIM]
                    pe.matmul(o, ones_bf[:], of_layer(b2s, c12, 0, DIM), start=True, stop=False)
                    for c in range(3):
                        m = pe.matmul(o, gT[:, c, :], of_layer(w2, c12, DIM * c, DIM * (c + 1)),
                                      start=False, stop=(c == 2))
                    m.then_inc(pe_w2, 1)

            def rec_gates(q, u):
                bank, gbank = (B2, B3)[u], (B01, B45)[u]
                pe.wait_ge(ac_lr_in, q + 1)
                pe.wait_ge(ac_lr_nT, due(q - 1))
                for t in range(TPS):
                    m = pe.transpose(bank[:, P * t:P * (t + 1)], R_in[u][:, P * t:P * (t + 1)], ident)
                m.then_inc(pe_lr_nT, 1)
                pe.wait_ge(ac_lr_nT, q + 1)
                pe.wait_ge(ac_lr_g, due(q - 1))
                for n in range(2):
                    m = pe.matmul(gbank[:, TOKENS * n:TOKENS * (n + 1)], gate_w[:, n, :], R_nT[u],
                                  start=True, stop=True)
                m.then_inc(pe_lr_g, 1)

            def rec_back(q, u):
                pe.wait_ge(dv_lr_h, q + 1)
                pe.wait_ge(dv_lr_x, due(q - 1))
                for t in range(TPS):
                    m = pe.transpose((B6, B7)[u][:, P * t:P * (t + 1)], R_w[u][:, P * t:P * (t + 1)], ident)
                m.then_inc(pe_lr_h, 1)

            barrier(pe, 1)
            pipeline(pe, slot, 0)
            barrier(pe, 2)
            rec_gates(0, 0)

            def step(q, u):
                if within(q, 0, SEQS - 2):
                    rec_gates(q + 1, 1 - u)
                if within(q, 2, SEQS - 1):
                    rec_back(q - 2, u)

            recurrence(pe, step)
            rec_back(SEQS - 2, 0)
            rec_back(SEQS - 1, 1)
            barrier(pe, 3)
            pipeline(pe, slot, 1)

        @block.scalar
        def _(act):
            def copy(out_, in_):
                return act.activation(out_, in_, ACT.Copy)

            table_turn = count()

            def fetch_table(function):
                n = next(table_turn) % 8
                act.activation(table_scratch[:, n:n + 1], half_neg[:, 0:1], function)

            def exps(st, e):
                for j in range(4):
                    h = 4 * e + j
                    m = act.activation(S[:, st.par, e, j, :], S[:, st.par, e, j, :], ACT.Exp,
                                       bias=nmx[:, st.par, h:h + 1], accum_out=rsum[:, st.par, h:h + 1])
                m.then_inc(ac_P, 1)

            def slot(call, it, t, steady, at):
                g, a1, a2, a3, c11, c12 = (at(n) for n in (0, 1, 2, 3, 11, 12))
                k = g.k
                if g.live:
                    act.wait_ge(pe_qk, N(call, k))
                    act.wait_ge(dv_ss, N(call, k - 1))
                    for n in range(2):
                        act.activation(sq[:, 512 * n:512 * (n + 1)], B01[:, 512 * n:512 * (n + 1)], ACT.Square)\
                            .then_inc(ac_sq, 1)
                    act.wait_ge(pe_v, N(call, k))
                    act.wait_ge(pe_O, N(call, k - 4, 2, 2))
                    copy(Vb[:, g.r], B2[:].rearrange("p (h d) -> p h d", h=HEADS)).then_inc(ac_v, 1)
                if a1.live:
                    act.wait_ge(pe_qT, N(call, a1.k))
                    act.wait_ge(pe_S, N(call, a1.k - 4))
                    copy(QT[:, :, a1.r, :], B3[:].rearrange("p (c n) -> p c n", c=4)).then_inc(ac_qT, 1)
                if a3.live:
                    exps(a3, 1)
                if a1.live:
                    act.wait_ge(pe_kT, N(call, a1.k))
                    act.wait_ge(pe_S, N(call, a1.k - 3))
                    copy(KT[:, :, a1.r, :], B3[:].rearrange("p (c n) -> p c n", c=4)).then_inc(ac_kT, 1)

                def probs_T(e):
                    act.wait_ge(pe_PT, N(call, a3.k, 2, 1 + e))
                    act.wait_ge(pe_O, N(call, a3.k - 1, 2, 1 + e))
                    copy(PT[:, e].rearrange("p j n -> p (j n)"), B6[:]).then_inc(ac_PT, 1)

                if a3.live:
                    probs_T(0)
                if c11.live:
                    fetch_table(ACT.Gelu)
                    act.wait_ge(pe_h, N(call, c11.k))
                    act.wait_ge(dv_gg, N(call, c11.k - 1))
                    act.activation(gl[:], B01[:, 512:512 + HID], ACT.Gelu).then_inc(ac_gl, 1)
                if a3.live:
                    probs_T(1)
                if c12.live:
                    act.wait_ge(pe_gT, N(call, c12.k))
                    act.wait_ge(pe_w2, N(call, c12.k - 1))
                    copy(gT[:].rearrange("p c n -> p (c n)"), B3[:, 0:3 * P]).then_inc(ac_gT, 1)
                if a2.live:
                    fetch_table(ACT.Exp)
                if a3.live:
                    act.wait_ge(pe_O, N(call, a3.k, 2, 2))
                    act.wait_ge(pe_wo, N(call, a3.k - 2))
                    copy(OT[:, a3.par].rearrange("p c n -> p (c n)"), B7[:]).then_inc(ac_OT, 1)
                if a2.live:
                    act.wait_ge(dv_sm, N(call, a2.k))
                    exps(a2, 0)

            def rec_in(q, u):
                act.wait_ge(dv_y, SEQS * TPS + TILES + TPS * q + TPS)
                act.wait_ge(pe_lr_nT, due(q - 1))
                y = ys[:, q] if isinstance(q, int) else ys[:, bass.ds(q, 1)].rearrange("p a t d -> p (a t) d")
                copy(R_in[u].rearrange("p (t d) -> p t d", t=TPS), y).then_inc(ac_lr_in, 1)

            def rec_nT(q, u):
                act.wait_ge(pe_lr_nT, q + 1)
                act.wait_ge(po_lr_nx, due(q - 1))
                copy(R_nT[u], (B2, B3)[u][:]).then_inc(ac_lr_nT, 1)

            def rec_gates(q, u):
                act.wait_ge(pe_lr_g, q + 1)
                act.wait_ge(dv_lr_w, due(q - 1))
                gbank = (B01, B45)[u]
                act.activation(R_gx[u], gbank[:, 0:TOKENS], ACT.Sigmoid, bias=gate_b[:, 0:1])
                act.activation(R_ga[u], gbank[:, TOKENS:2 * TOKENS], ACT.Sigmoid, bias=gate_b[:, 1:2])\
                    .then_inc(ac_lr_g, 1)
                act.wait_ge(ac_lr_g, q + 1)
                act.wait_ge(dv_lr_p, due(q - 1))
                act.activation(R_a[u], R_ga[u], ACT.Exp, scale=decay[:, 0:1])
                act.wait_ge(ac_lr_m, due(q - 1))
                act.activation(R_a2[u], R_ga[u], ACT.Exp, scale=decay[:, 1:2]).then_inc(ac_lr_a, 1)
                act.wait_ge(dv_lr_m, q + 1)
                act.wait_ge(po_lr_nm, due(q - 1))
                act.activation(R_mult[u], R_a2[u], ACT.Sqrt, scale=-1.0).then_inc(ac_lr_m, 1)

            barrier(act, 1)
            pipeline(act, slot, 0)
            barrier(act, 2)
            rec_in(0, 0)
            rec_in(1, 1)
            rec_nT(0, 0)

            def step(q, u):
                if within(q, 0, SEQS - 2):
                    rec_nT(q + 1, 1 - u)
                rec_gates(q, u)
                if within(q, 0, SEQS - 3):
                    rec_in(q + 2, u)

            recurrence(act, step)
            barrier(act, 3)
            pipeline(act, slot, 1)

        @block.gpsimd
        def _(pool):
            def inverse_std(n, u):
                pool.wait_ge(dv_pst, n + 1)
                pool.tensor_tensor(prs[:, u], pmv[:, u, :, 1], half_neg[:, 0:TPS], ALU.pow).then_inc(po_prs, 1)

            def prepass(first):
                with pool.Fori(0, SEQS // 2) as i:
                    inverse_std(first + 2 * i, 0)
                    inverse_std(first + 2 * i + 1, 1)

            def slot(call, it, t, steady, at):
                g, a3, nxt = at(0), at(3), at(-1)
                def over_sum(e):
                    pool.wait_ge(dv_rinv, N(call, a3.k, 2, 1 + e))
                    s4 = S[:, a3.par, e]
                    pool.tensor_tensor(s4, s4, rinv[:, a3.par, 4 * e:4 * e + 4].unsqueeze(2).broadcast_to([P, 4, P]),
                                       ALU.mult).then_inc(po_P, 1)

                if a3.live:
                    over_sum(0)
                if nxt.live:
                    pool.wait_ge(dv_y, YCALL * call + nxt.k + 1)
                    pool.wait_ge(pe_yT, N(call, nxt.k - 2))
                    pool.tensor_copy(yst[:, nxt.par, :], tile_of(ys, nxt)).then_inc(po_y, 1)
                if g.live:
                    k = g.k
                    c4 = rot[:, g.par].rearrange("p (h f d) -> p h f d", f=2, d=DH // 2)
                    s4 = rsin[:, g.par].rearrange("p (h f d) -> p h f d", f=2, d=DH // 2)
                    for n in range(2):
                        pool.wait_ge(dv_rope, N(call, k, 2, 1 + n))
                        heads = slice(HEADS * n, HEADS * (n + 1))
                        pool.tensor_tensor(c4[:, heads], c4[:, heads], s4[:, heads, 1::-1, :], ALU.add)\
                            .then_inc(po_add, 1)
                if a3.live:
                    over_sum(1)
                if g.live:
                    pool.wait_ge(po_q, N(call, k - 2))
                    pool.wait_ge(dv_ss, N(call, k))
                    pool.tensor_tensor(rn[:, g.par], ss[:, g.par], half_neg[:], ALU.pow).then_inc(po_rn, 1)
                    pool.wait_ge(po_add, N(call, k, 2, 2))
                    pool.wait_ge(po_rn, N(call, k))
                    c3 = rot[:, g.par].rearrange("p (h d) -> p h d", d=DH)
                    pool.tensor_tensor(c3, c3, rn[:, g.par].unsqueeze(2).broadcast_to([P, 2 * HEADS, DH]), ALU.mult)\
                        .then_inc(po_q, 1)
                if t == 0 and seq_live(it):
                    j = it - 2
                    pool.wait_ge(dv_ag, J(call, j))
                    pool.tensor_tensor(mr[:, 0:TPS, 1], mv[:, :, 1], half_neg[:, 0:TPS], ALU.pow).then_inc(po_rs, 1)

            def rec_products(q, u):
                pool.wait_ge(ac_lr_g, q + 1)
                pool.tensor_tensor(R_gx[u], R_gx[u], R_nT[u], ALU.mult).then_inc(po_lr_nx, 1)
                pool.wait_ge(po_lr_nx, q + 1)
                pool.wait_ge(ac_lr_m, q + 1)
                pool.tensor_tensor(R_gx[u], R_gx[u], R_mult[u], ALU.mult).then_inc(po_lr_nm, 1)

            pool.wait_ge(set_v, 1)
            prepass(0)
            pool.wait_ge(set_d, 2 * LAYERS + 4)
            pool.tensor_tensor(decay[:, 4:5], decay[:, 3:4], decay[:, 2:3], ALU.pow).then_inc(set_p, 1)
            barrier(pool, 1)
            pipeline(pool, slot, 0)
            barrier(pool, 2)
            for q in range(AHEAD + 1):
                inverse_std(SEQS + q, q % 2)

            def step(q, u):
                rec_products(q, u)
                if within(q, 0, SEQS - 2 - AHEAD):
                    inverse_std(SEQS + AHEAD + 1 + q, 1 - u)

            recurrence(pool, step)
            barrier(pool, 3)
            prepass(2 * SEQS)
            pipeline(pool, slot, 1)

        @block.vector
        def _(dve):
            links = [0]

            def link(ins):
                links[0] += 1
                ins.then_inc(set_d, 1)
                dve.wait_ge(set_d, links[0])

            def norm_stats(first, q, u):
                for t in range(TPS):
                    m = dve.bn_stats(pst[:, u, t, :], seq_tile(xs, q, t))
                m.then_inc(dv_pa, 1)
                dve.wait_ge(dv_pa, first + q + 1)
                settle(dve)
                for t in range(TPS):
                    m = dve.bn_aggr(pmv[:, u, t, :], pst[:, u, t, :])
                m.then_inc(dv_pag, 1)
                dve.wait_ge(dv_pag, first + q + 1)
                dve.tensor_scalar(pmv[:, u, :, 1], pmv[:, u, :, 1], EPS, None, ALU.add).then_inc(dv_pst, 1)

            def norm_apply(first, q, u):
                dve.wait_ge(po_prs, first + q + 1)
                for t in range(TPS):
                    dve.tensor_scalar(seq_tile(ys, q, t), seq_tile(xs, q, t), pmv[:, u, t, 0:1],
                                      prs[:, u, t:t + 1], ALU.subtract, ALU.mult).then_inc(dv_y, 1)

            def prepass(first):
                norm_stats(first, 0, 0)
                norm_stats(first, 1, 1)
                norm_apply(first, 0, 0)
                with dve.Fori(1, SEQS // 2) as i:
                    norm_stats(first, 2 * i, 0)
                    norm_apply(first, 2 * i - 1, 1)
                    norm_stats(first, 2 * i + 1, 1)
                    norm_apply(first, 2 * i, 0)
                norm_apply(first, SEQS - 1, 1)

            def setup():
                dve.memset(w2[:, :, 2, :], 0.0)
                dve.memset(gate_w[:], 0.0)
                dve.memset(b1s[:], 0.0)
                dve.memset(b2s[:], 0.0)
                dve.memset(ones_bf[:], 1.0)
                dve.memset(mT[:], 0.0)
                dve.memset(Vb[:], 0.0)
                dve.memset(Va[:], 0.0)
                dve.memset(gg[:], 0.0)
                dve.memset(mr[:], 0.0)
                dve.memset(half_neg[:], -0.5)
                dve.memset(decay[:, 3:4], float(np.e))
                for c, v in enumerate((32.0, 0.0, 0.0, 32.0, 0.0, 0.0)):
                    m = dve.memset(tupB[:, 0, c:c + 1], v)
                m.then_inc(set_v, 1)
                dve.wait_ge(load_x, 64)
                prepass(0)
                dve.wait_ge(load_w, W_ALL)
                dve.wait_ge(set_v, 1)
                dve.tensor_copy(hT[64:128, 0:1], mT[64:128, 0:1])
                dve.tensor_copy(hT_lo[64:128, 0:1], mT[64:128, 0:1])
                for l in range(LAYERS):
                    link(dve.tensor_copy(wqkv_hi[:, l], w_in[l]))
                    link(dve.tensor_tensor(wqkv_lo[:, l], w_in[l], wqkv_hi[:, l], ALU.subtract))
                dve.memset(KT[:], 0.0)
                link(dve.tensor_scalar(decay[:, 5:6], decay[:, 0:1], -1.0, None, ALU.mult))
                link(dve.tensor_tensor(decay[:, 2:3], decay[:, 0:1], decay[:, 5:6], ALU.min))
                for l in range(LAYERS):
                    v = rope[:, l].rearrange("p a t n d -> p (a t) (n d)")
                    link(dve.tensor_tensor(v, v, qk_scale[:, l:l + 1].rearrange("p a n d -> p a (n d)")
                                           .broadcast_to([P, 2 * TPS, 2 * DH]), ALU.mult))
                for l in range(LAYERS):
                    m = dve.tensor_copy(PT[:, 0, l, 0:3], lnp_w[:, l, 1:2].broadcast_to([P, 3]))
                m.then_inc(set_v, 1)
                dve.wait_ge(set_e, 1)

                def three_parts(dst, b, f, h):
                    n = b.shape[-1]
                    hb = h.bitcast(BF16)
                    for part in range(3):
                        link(dve.tensor_copy(hb[:, part * n:(part + 1) * n], b))
                        if part < 2:
                            link(dve.tensor_tensor(b, b, hb[:, part * n:(part + 1) * n], ALU.subtract))
                    link(dve.tensor_scalar(f, hb[:, 0:n], cst[0:3, C_IDENT:C_IDENT + 1], None, ALU.mult))
                    link(dve.scalar_tensor_tensor(out=f, in0=hb[:, n:2 * n], scalar=cst[0:3, C_IDENT + 1:C_IDENT + 2],
                                                  in1=f, op0=ALU.mult, op1=ALU.add))
                    link(dve.scalar_tensor_tensor(out=dst, in0=hb[:, 2 * n:3 * n],
                                                  scalar=cst[0:3, C_IDENT + 2:C_IDENT + 3],
                                                  in1=f, op0=ALU.mult, op1=ALU.add))

                for l in range(LAYERS):
                    link(dve.tensor_scalar(w1[:, l], w1[:, l], lnp_w[:, l, 0:1], None, ALU.mult))
                    b = sq[0:3, 0:2 * HID] if l == 0 else rot[0:3, 0, 0:2 * HID]
                    bv = b.rearrange("p (n c) -> p n c", n=2)
                    made = (B01 if l == 0 else B45)[0:3].rearrange("p (n c) -> p n c", n=2)[:, :, 0:HID]
                    link(dve.tensor_tensor(bv, made, bv, ALU.add))
                    three_parts(b1s[0:3, l], b, rot[0:3, 1, 0:2 * HID], S[0:3].rearrange("p a e j n -> p (a e j n)"))
                    three_parts(b2s[0:3, l], rsin[0:3, 0, l * DIM:(l + 1) * DIM], rot[0:3, 1, 0:DIM],
                                S[0:3].rearrange("p a e j n -> p (a e j n)"))
                dve.wait_ge(set_p, 1)
                z, w, sc, s2, p = (decay[:, n:n + 1] for n in (4, 5, 6, 7, 2))
                link(dve.tensor_scalar(w, z, 2.0, None, ALU.add))
                link(dve.reciprocal(w, w))
                link(dve.tensor_tensor(sc, z, w, ALU.mult))
                link(dve.tensor_tensor(s2, sc, sc, ALU.mult))
                link(dve.memset(p, 1.0 / 21))
                for n in range(19, 0, -2):
                    link(dve.tensor_scalar(p, p, s2, 1.0 / n, ALU.mult, ALU.add))
                link(dve.tensor_tensor(p, p, sc, ALU.mult))
                link(dve.tensor_scalar(w, decay[:, 0:1], 0.0, None, ALU.max))
                link(dve.scalar_tensor_tensor(out=w, in0=p, scalar=2.0, in1=w, op0=ALU.mult, op1=ALU.add))
                link(dve.tensor_scalar(decay[:, 0:1], w, -8.0, None, ALU.mult))
                link(dve.tensor_scalar(decay[:, 1:2], w, -16.0, None, ALU.mult))
                dve.sem_inc(set_v, 1)

            def slot(call, it, t, steady, at):
                g, a1, a2, a3, a4 = (at(n) for n in range(5))
                nxt, c9, c10, c11, c12 = (at(n) for n in (-1, 9, 10, 11, 12))
                k = g.k
                def invert_sum(e):
                    dve.wait_ge(ac_P, N(call, a3.k, 2, 1 + e))
                    dve.wait_ge(po_P, N(call, a3.k - 2, 2, 2))
                    dve.reciprocal(rinv[:, a3.par, 4 * e:4 * e + 4], rsum[:, a3.par, 4 * e:4 * e + 4])\
                        .then_inc(dv_rinv, 1)

                if a3.live:
                    invert_sum(0)
                if g.live:
                    dve.wait_ge(pe_kT, N(call, k - 2))
                    for n in range(2):
                        dve.wait_ge(ac_sq, N(call, k, 2, 1 + n))
                        q3 = B01[:, 512 * n:512 * (n + 1)].rearrange("p (h d) -> p h d", d=DH)
                        for cs, buf in enumerate((rot, rsin)):
                            m = dve.tensor_tensor(
                                buf[:, g.par, 512 * n:512 * (n + 1)].rearrange("p (h d) -> p h d", d=DH), q3,
                                rope_of(g, cs, n), ALU.mult)
                        m.then_inc(dv_rope, 1)
                if g.live:
                    dve.wait_ge(po_rn, N(call, k - 2))
                    dve.tensor_reduce(ss[:, g.par], sq[:].rearrange("p (h d) -> p h d", d=DH), AX.X, ALU.add)\
                        .then_inc(dv_sum, 1)
                    dve.wait_ge(dv_sum, N(call, k))
                    dve.tensor_scalar(ss[:, g.par], ss[:, g.par], 1e-24, None, ALU.max).then_inc(dv_ss, 1)
                if a3.live:
                    invert_sum(1)
                if a2.live:
                    dve.wait_ge(pe_S, N(call, a2.k))
                    dve.wait_ge(pe_PT, N(call, a2.k - 2, 2, 2))
                    settle(dve)
                    mask = cst[:, C_MASK + (0 if a2.r == 0 else P):][:, 0:P]
                    for e in range(2):
                        for j in range(4):
                            h = 2 * j + e
                            m = dve.tensor_tensor_reduce(S[:, a2.par, j // 2, h % 4, :],
                                                         B45[:, 512 * e + P * j:][:, 0:P], mask,
                                                         1.0, LOWEST, ALU.add, ALU.max, mx[:, a2.par, h:h + 1])
                    m.then_inc(dv_mx, 1)
                    dve.wait_ge(dv_mx, N(call, a2.k))
                    dve.tensor_scalar(nmx[:, a2.par], mx[:, a2.par], -1.0, None, ALU.mult).then_inc(dv_sm, 1)
                if c11.live:
                    dve.wait_ge(ac_gl, N(call, c11.k))
                    dve.wait_ge(pe_gT, N(call, c11.k - 2))
                    dve.tensor_tensor(gg[:, c11.par, 0:HID], B01[:, 0:HID], gl[:], ALU.mult).then_inc(dv_gg, 1)

                def shifted(dst, st, src):
                    c = P * st.r
                    dve.tensor_copy(dst[0:64, c:c + P], src[0:64, :])
                    return dve.tensor_copy(dst[64:128, c + 1:c + P + 1], src[64:128, :])

                if nxt.live:
                    dve.wait_ge(pe_yT, N(call, nxt.k))
                if c10.live:
                    dve.wait_ge(pe_nT, N(call, c10.k))
                if nxt.live:
                    shifted(hT, nxt, B2[:, 0:P]).then_inc(dv_hh, 1)
                if c10.live:
                    if c10.r == 0:
                        dve.tensor_copy(mT[64:128, 0:1], B2[64:128, 2 * P:2 * P + 1])
                    shifted(mT, c10, B2[:, P:2 * P]).then_inc(dv_mT, 1)
                if nxt.live:
                    dve.wait_ge(dv_hh, N(call, nxt.k))
                    for rows, on in ((slice(0, 64), 0), (slice(64, 128), 1)):
                        c = slice(P * nxt.r + on, P * nxt.r + on + P)
                        m = dve.tensor_tensor(hT_lo[rows, c], B2[rows, 0:P], hT[rows, c], ALU.subtract)
                    m.then_inc(dv_hT, 1)
                if t == 1 and seq_live(it):
                    j = it - 2
                    dve.wait_ge(pe_st2, J(call, j))
                    dve.tensor_copy(lnp[:, :, 0, :], mr[:, 0:TPS, :])
                    dve.tensor_copy(lnp[:, :, 1, :], B45[:, 512:512 + 2 * TPS].rearrange("p (t n) -> p t n", n=2))\
                        .then_inc(dv_lp, 1)
                    dve.wait_ge(dv_lp, J(call, j))
                    dve.scalar_tensor_tensor(out=before[:], in0=lnp[:, 0, 0, 0:1].broadcast_to([P, 2]), scalar=-1.0,
                                             in1=lnp[:, 0, 0, 1:2].broadcast_to([P, 2]), op0=ALU.mult, op1=ALU.mult)
                if a4.live:
                    dve.wait_ge(pe_wo, N(call, a4.k))
                    y = tile_of(ys, a4)
                    dve.tensor_tensor(y, wo_out(t), y, ALU.add).then_inc(dv_r1, 1)
                if c9.live:
                    dve.wait_ge(dv_lp, J(call, (c9.k - c9.r) // TPS if isinstance(c9.k, int) else it + c9.back))
                    dve.wait_ge(dv_r1, N(call, c9.k))
                    y = tile_of(ys, c9)
                    for f in range(2):
                        m = dve.tensor_scalar(nb[:, c9.r, 64 * f:64 * f + 64], y[:, 64 * f:64 * f + 64],
                                              lnp[:, c9.r, f, 0:1], lnp[:, c9.r, f, 1:2], ALU.subtract, ALU.mult)
                    m.then_inc(dv_ln, 1)
                def half_stats():
                    dve.wait_ge(dv_r1, N(call, a4.k))
                    settle(dve)
                    y = tile_of(ys, a4)
                    dve.bn_stats(tup[:, a4.r, 0:6], y[:, 0:64])
                    dve.bn_stats(tupB[:, a4.r + 1, :], y[:, 64:128]).then_inc(dv_bn, 1)

                if a4.live and t != 0:
                    half_stats()
                if c12.live:
                    dve.wait_ge(pe_w2, N(call, c12.k))
                    y = tile_of(ys, c12)
                    dve.tensor_tensor(y, B2[:, 0:DIM], y, ALU.add).then_inc(dv_y, 1)
                if t == 0 and seq_live(it):
                    j = it - 2
                    dve.wait_ge(pe_st1, J(call, j))
                    dve.tensor_copy(tup[:, :, 6:12], B45[:, 0:TPS * 6].rearrange("p (t n) -> p t n", n=6))\
                        .then_inc(dv_tc, 1)
                    dve.wait_ge(dv_tc, J(call, j))
                    dve.wait_ge(dv_bn, N(call, TPS * j + TPS - 1))
                    dve.wait_ge(po_rs, J(call, j - 1))
                    settle(dve)
                    for r in range(TPS):
                        m = dve.bn_aggr(mv[:, r, :], tup[:, r, :])
                    m.then_inc(dv_agg, 1)
                    dve.wait_ge(dv_agg, J(call, j))
                    dve.tensor_scalar(mr[:, 0:TPS, 0], mv[:, :, 0], 0.0, None, ALU.add)
                    dve.tensor_scalar(mv[:, :, 1], mv[:, :, 1], EPS, None, ALU.add).then_inc(dv_ag, 1)
                if a4.live and t == 0:
                    half_stats()
                if a1.live:
                    dve.wait_ge(ac_v, N(call, a1.k))
                    dve.wait_ge(pe_O, N(call, a1.k - 3, 2, 2))
                    dve.tensor_copy(Va[0:64, a1.r], Vb[0:64, a1.r])
                    dve.tensor_copy(Va[64:128, (a1.r + 1) % TPS], Vb[64:128, a1.r])\
                        .then_inc(dv_vc, 1)

            def block_residual(call):
                dve.wait_ge(dv_y, Y(call, TILES - 1))
                for q in range(4):
                    x = xs[:, 4 * q:4 * q + 4].rearrange("p s t d -> p (s t d)")
                    y = ys[:, 4 * q:4 * q + 4].rearrange("p s t d -> p (s t d)")
                    dve.scalar_tensor_tensor(out=x, in0=y, scalar=0.5, in1=x, op0=ALU.mult, op1=ALU.add)\
                        .then_inc(dv_x, 1)

            def rec_clip(q, u):
                dve.wait_ge(ac_lr_a, q + 1)
                dve.tensor_scalar(R_a2[u], R_a2[u], 1.0, -1e-7, ALU.subtract, ALU.min).then_inc(dv_lr_m, 1)

            def rec_scan(q, u):
                zero = zero_col[:].broadcast_to([P, TOKENS])
                dve.tensor_tensor_scan(R_p[u][:, 1:TOKENS + 1], R_a[u], zero, 1.0, ALU.mult, ALU.add)\
                    .then_inc(dv_lr_p, 1)
                dve.wait_ge(dv_lr_p, q + 1)
                dve.tensor_scalar(R_pc[u], R_p[u][:, 0:TOKENS], 1e-7, None, ALU.max).then_inc(dv_lr_pc, 1)
                dve.wait_ge(dv_lr_pc, q + 1)
                dve.reciprocal(R_rec[u], R_pc[u]).then_inc(dv_lr_rec, 1)
                dve.wait_ge(dv_lr_rec, q + 1)
                dve.wait_ge(po_lr_nm, q + 1)
                dve.wait_ge(pe_lr_h, due(q - 1))
                dve.tensor_tensor(R_w[u], R_gx[u], R_rec[u], ALU.mult).then_inc(dv_lr_w, 1)
                dve.wait_ge(dv_lr_w, q + 1)
                dve.tensor_tensor_scan(R_S[u], R_w[u], zero, 0.0, ALU.add, ALU.add).then_inc(dv_lr_S, 1)
                dve.wait_ge(dv_lr_S, q + 1)
                dve.tensor_tensor(R_w[u], R_pc[u], R_S[u], ALU.mult).then_inc(dv_lr_h, 1)

            def rec_add(q, u):
                dve.wait_ge(pe_lr_h, q + 1)
                x = xs[:, q] if isinstance(q, int) else xs[:, bass.ds(q, 1)].rearrange("p a t d -> p (a t) d")
                dve.tensor_tensor(x, (B6, B7)[u][:].rearrange("p (t d) -> p t d", t=TPS), x, ALU.add)\
                    .then_inc(dv_lr_x, 1)

            setup()
            barrier(dve, 1)
            pipeline(dve, slot, 0)
            block_residual(0)
            barrier(dve, 2)
            dve.wait_ge(dv_x, 4)
            for u in turns:
                dve.memset(R_p[u][:, 0:1], 1.0)
            dve.memset(zero_col[:], 0.0).then_inc(dv_z, 1)
            dve.wait_ge(dv_z, 1)
            norm_stats(SEQS, 0, 0)
            for q in range(AHEAD):
                norm_stats(SEQS, q + 1, (q + 1) % 2)
                norm_apply(SEQS, q, q % 2)
            rec_clip(0, 0)

            def step(q, u):
                if within(q, 0, SEQS - 2 - AHEAD):
                    norm_stats(SEQS, q + AHEAD + 1, 1 - u)
                if within(q, 0, SEQS - 2):
                    rec_clip(q + 1, 1 - u)
                rec_scan(q, u)
                if within(q, 0, SEQS - 1 - AHEAD):
                    norm_apply(SEQS, q + AHEAD, u)
                if within(q, 2, SEQS - 1):
                    rec_add(q - 2, u)

            recurrence(dve, step)
            rec_add(SEQS - 2, 0)
            rec_add(SEQS - 1, 1)
            barrier(dve, 3)
            dve.wait_ge(dv_lr_x, SEQS)
            prepass(2 * SEQS)
            pipeline(dve, slot, 1)
            block_residual(1)


_INS = ["L0_attn_x", "L0_attn_ig_w", "L0_attn_ig_b", "L0_attn_ag_w", "L0_attn_ag_b", "L0_attn_a_param", "L0_ffn_wqkv",
        "L0_ffn_q_scale", "L0_ffn_k_scale", "L0_ffn_wo", "L0_ffn_ln_g", "L0_ffn_ln_b", "L0_ffn_w1", "L0_ffn_b1",
        "L0_ffn_w2", "L0_ffn_b2"]


def kernel(**inputs):
    import numpy as _np
    import concourse.bacc as _bacc
    from concourse import mybir as _mybir
    from concourse.bass_utils import run_bass_kernel_spmd as _run

    nc = _bacc.Bacc("TRN2", target_bir_lowering=False, num_devices=1)
    arrays, args = {}, []
    for name in _INS:
        arrays[f"in_{name}"] = _np.ascontiguousarray(inputs[name])
    arrays["in_consts"] = shape_constants()
    for name, a in arrays.items():
        args.append(nc.dram_tensor(name, a.shape, _mybir.dt.from_np(a.dtype), kind="ExternalInput").ap())
    args.append(nc.dram_tensor("out_0", (SEQS, TOKENS, DIM), _mybir.dt.float32, kind="ExternalOutput").ap())
    build(nc, *args)
    r = _run(nc, [arrays], core_ids=[0])
    return r.results[0]["out_0"]
```
